# Optimizing a Trainium2 kernel written in Bass

```python
import numpy as np
import jax
import jax.numpy as jnp

def _softmax(x, axis=-1):
    return jax.nn.softmax(x, axis=axis)

def _gelu(x):
    return jax.nn.gelu(x, approximate=True)

def _silu(x):
    return jax.nn.silu(x)

def _sigmoid(x):
    return jax.nn.sigmoid(x)

def _layernorm(x, axis=-1, eps=1e-05):
    m = jnp.mean(x, axis=axis, keepdims=True)
    v = jnp.var(x, axis=axis, keepdims=True)
    return (x - m) / jnp.sqrt(v + eps)

def _scatter_add(tgt, idx, src, axis=0):
    return tgt.at[idx].add(src)

def _segment_sum(src, seg, n):
    return jax.ops.segment_sum(src, seg, n)
kernel_name = 'mk_early_fusion_embed_d2_tok_img768_r4_f64e65'

def setup_inputs(seed: int=0):
    np.random.seed(seed)
    _w = jnp.asarray

    def _rec_inputs():
        import jax
        import jax.numpy as jnp
        _rk = jax.random.key(seed)
        x = -0.000125008 + 0.999885 * jax.random.normal(jax.random.fold_in(_rk, 1), (8, 2, 128, 128), jnp.float32)
        x_txt = jax.random.randint(jax.random.fold_in(_rk, 51), (8, 128), 0, 31999, jnp.int32)
        mask_BS_i2_0 = jnp.where(jnp.ones((8, 128), dtype=bool), 2, 0).astype(jnp.int32)
        return (x, x_txt, mask_BS_i2_0)
    x, x_txt, mask_BS_i2_0 = _rec_inputs()

    def _L0_tok_setup():
        import jax, jax.numpy as jnp
        import numpy as np
        PATCH = 16

        def _patchify(x, p):
            B, C, H, W = x.shape
            nh, nw = (H // p, W // p)
            patch_dim = C * p * p
            x = x.reshape(B, C, nh, p, nw, p)
            x = jnp.transpose(x, (0, 1, 2, 4, 3, 5))
            return x.reshape(B, -1, patch_dim)
        key = jax.random.key(seed)
        k1, k2, k3, k4 = jax.random.split(key, 4)
        B, C, H, W = (64, 2, 128, 128)
        dim = 192
        num_patches = H // PATCH * (W // PATCH)
        patch_dim = C * PATCH * PATCH
        x = jax.random.normal(k1, (B, C, H, W), dtype=jnp.float32)
        proj_w = jax.random.normal(k2, (dim, patch_dim), dtype=jnp.float32) * 0.02
        proj_b = jax.random.normal(k3, (dim,), dtype=jnp.float32) * 0.02
        pos_emb = jax.random.normal(k4, (1, num_patches, dim), dtype=jnp.float32) * 0.02
        return {'x': x, 'proj_w': proj_w, 'proj_b': proj_b, 'pos_emb': pos_emb}
    _L0_tok_all = _L0_tok_setup()
    _L0_tok_in = {k: v for k, v in _L0_tok_all.items() if k in ('proj_w', 'proj_b', 'pos_emb')}
    del _L0_tok_all

    def _L0_txt_setup():
        import jax, jax.numpy as jnp
        import numpy as np
        VOCAB = 8000
        DIM = 192
        BATCH = 8
        SEQ = 512

        def _sinusoidal_pos(seq_len, dim):
            pos = jnp.arange(seq_len, dtype=jnp.float32)[:, None]
            ids = jnp.arange(dim, dtype=jnp.float32)[None, :]
            even_exp = jnp.floor(ids / 2.0) * 2.0 / dim
            angle = pos / jnp.power(10000.0, even_exp)
            return jnp.where(jnp.arange(dim) % 2 == 0, jnp.sin(angle), jnp.cos(angle))
        key = jax.random.key(seed)
        k1, k2, k3, k4 = jax.random.split(key, 4)
        input_tensor = jax.random.randint(k1, (BATCH, SEQ), 0, VOCAB)
        segment_label = jax.random.randint(k2, (BATCH, SEQ), 0, 3)
        token_table = jax.random.normal(k3, (VOCAB, DIM), dtype=jnp.float32) * 0.02
        segm_table = jax.random.normal(k4, (3, DIM), dtype=jnp.float32) * 0.02
        token_table = token_table.at[0].set(0.0)
        segm_table = segm_table.at[0].set(0.0)
        return {'input_tensor': input_tensor, 'segment_label': segment_label, 'token_table': token_table, 'segm_table': segm_table}
    _L0_txt_all = _L0_txt_setup()
    _L0_txt_in = {k: v for k, v in _L0_txt_all.items() if k in ('token_table', 'segm_table')}
    del _L0_txt_all

    def _L0_attn_setup():
        import jax, jax.numpy as jnp
        import numpy as np
        B, T, D = (8, 1024, 192)
        BS = 3
        NB = D // BS

        def _rodrigues(b, v):
            theta = jnp.linalg.norm(b, axis=-1, keepdims=True)
            k = b / jnp.maximum(theta, 1e-08)
            c = jnp.cos(theta)
            s = jnp.sin(theta)
            cross = jnp.cross(k, v)
            dot = jnp.sum(k * v, axis=-1, keepdims=True)
            return v * c + cross * s + k * dot * (1.0 - c)
        key = jax.random.key(seed)
        ks = jax.random.split(key, 6)
        s = 1.0 / np.sqrt(D)
        return {'x_seq': jax.random.normal(ks[0], (B, T, D), jnp.float32), 'W_biv': jax.random.uniform(ks[1], (NB * 3, D), jnp.float32, -s, s), 'b_biv': jnp.zeros((NB * 3,), jnp.float32), 'W_decay': jax.random.uniform(ks[2], (1, D), jnp.float32, -s, s), 'b_decay': jnp.full((1,), 1.4, jnp.float32), 'W_in': jax.random.uniform(ks[3], (D, D), jnp.float32, -s, s), 'b_in': jax.random.uniform(ks[4], (D,), jnp.float32, -s, s)}
    _L0_attn_all = _L0_attn_setup()
    _L0_attn_in = {k: v for k, v in _L0_attn_all.items() if k in ('W_biv', 'b_biv', 'W_decay', 'b_decay', 'W_in', 'b_in')}
    del _L0_attn_all

    def _L0_ffn_setup():
        import jax, jax.numpy as jnp
        import numpy as np
        EMB = 192
        HID = 288
        NUM_EXPERTS = 8
        TOP_K = 2
        key = jax.random.key(seed)
        ks = jax.random.split(key, 8)
        s = 0.02
        x = jax.random.normal(ks[0], (4, 256, EMB), dtype=jnp.float32)
        router_w = jax.random.normal(ks[1], (EMB, NUM_EXPERTS), dtype=jnp.float32) * s
        router_b = jnp.zeros((NUM_EXPERTS,), dtype=jnp.float32)
        w1 = jax.random.normal(ks[2], (NUM_EXPERTS, EMB, HID), dtype=jnp.float32) * s
        b1 = jnp.zeros((NUM_EXPERTS, HID), dtype=jnp.float32)
        w2 = jax.random.normal(ks[3], (NUM_EXPERTS, HID, EMB), dtype=jnp.float32) * s
        b2 = jnp.zeros((NUM_EXPERTS, EMB), dtype=jnp.float32)
        return {'x': x, 'router_w': router_w, 'router_b': router_b, 'w1': w1, 'b1': b1, 'w2': w2, 'b2': b2}
    _L0_ffn_all = _L0_ffn_setup()
    _L0_ffn_in = {k: v for k, v in _L0_ffn_all.items() if k in ('router_w', 'router_b', 'w1', 'b1', 'w2', 'b2')}
    del _L0_ffn_all

    def _L1_attn_setup():
        import jax, jax.numpy as jnp
        import numpy as np
        B, N, C = (32, 256, 192)
        H = 12
        E = C // H
        SCALE = E ** (-0.5)
        EPS = 1e-06
        key = jax.random.key(seed)
        k1, k2, k3 = jax.random.split(key, 3)
        x = jax.random.normal(k1, (B, N, C), dtype=jnp.float32)
        qkv_w = jax.random.normal(k2, (3 * C, C), dtype=jnp.float32) * C ** (-0.5)
        proj_w = jax.random.normal(k3, (C, C), dtype=jnp.float32) * C ** (-0.5)
        proj_b = jnp.zeros((C,), dtype=jnp.float32)
        return {'x': x, 'qkv_w': qkv_w, 'proj_w': proj_w, 'proj_b': proj_b}
    _L1_attn_all = _L1_attn_setup()
    _L1_attn_in = {k: v for k, v in _L1_attn_all.items() if k in ('qkv_w', 'proj_w', 'proj_b')}
    del _L1_attn_all

    def _L1_ffn_setup():
        import jax, jax.numpy as jnp
        import numpy as np
        D_MODEL, D_FF, N_EXPERTS, TOP_K = (192, 768, 8, 2)
        B, S = (2, 256)
        LN_EPS = 1e-05

        def _layernorm(x, gamma, beta):
            mu = jnp.mean(x, axis=-1, keepdims=True)
            var = jnp.mean(jnp.square(x - mu), axis=-1, keepdims=True)
            return (x - mu) * jax.lax.rsqrt(var + LN_EPS) * gamma + beta
        key = jax.random.key(seed)
        k1, k2, k3, k4 = jax.random.split(key, 4)
        return {'hidden_states': jax.random.normal(k1, (B, S, D_MODEL), dtype=jnp.float32), 'ln_gamma': jnp.ones((D_MODEL,), dtype=jnp.float32), 'ln_beta': jnp.zeros((D_MODEL,), dtype=jnp.float32), 'router_w': jax.random.normal(k2, (D_MODEL, N_EXPERTS), dtype=jnp.float32) * 0.02, 'w1': jax.random.normal(k3, (N_EXPERTS, D_MODEL, D_FF), dtype=jnp.float32) * 0.02, 'w2': jax.random.normal(k4, (N_EXPERTS, D_FF, D_MODEL), dtype=jnp.float32) * 0.02}
    _L1_ffn_all = _L1_ffn_setup()
    _L1_ffn_in = {k: v for k, v in _L1_ffn_all.items() if k in ('ln_gamma', 'ln_beta', 'router_w', 'w1', 'w2')}
    del _L1_ffn_all
    return {'x': x, 'x_txt': x_txt, 'mask_BS_i2_0': mask_BS_i2_0, 'L0_tok_proj_w': _L0_tok_in['proj_w'], 'L0_tok_proj_b': _L0_tok_in['proj_b'], 'L0_tok_pos_emb': _L0_tok_in['pos_emb'], 'L0_txt_token_table': _L0_txt_in['token_table'], 'L0_txt_segm_table': _L0_txt_in['segm_table'], 'L0_attn_W_biv': _L0_attn_in['W_biv'], 'L0_attn_b_biv': _L0_attn_in['b_biv'], 'L0_attn_W_decay': _L0_attn_in['W_decay'], 'L0_attn_b_decay': _L0_attn_in['b_decay'], 'L0_attn_W_in': _L0_attn_in['W_in'], 'L0_attn_b_in': _L0_attn_in['b_in'], 'L0_ffn_router_w': _L0_ffn_in['router_w'], 'L0_ffn_router_b': _L0_ffn_in['router_b'], 'L0_ffn_w1': _L0_ffn_in['w1'], 'L0_ffn_b1': _L0_ffn_in['b1'], 'L0_ffn_w2': _L0_ffn_in['w2'], 'L0_ffn_b2': _L0_ffn_in['b2'], 'L1_attn_qkv_w': _L1_attn_in['qkv_w'], 'L1_attn_proj_w': _L1_attn_in['proj_w'], 'L1_attn_proj_b': _L1_attn_in['proj_b'], 'L1_ffn_ln_gamma': _L1_ffn_in['ln_gamma'], 'L1_ffn_ln_beta': _L1_ffn_in['ln_beta'], 'L1_ffn_router_w': _L1_ffn_in['router_w'], 'L1_ffn_w1': _L1_ffn_in['w1'], 'L1_ffn_w2': _L1_ffn_in['w2']}

def reference(x, x_txt, mask_BS_i2_0, L0_tok_proj_w, L0_tok_proj_b, L0_tok_pos_emb, L0_txt_token_table, L0_txt_segm_table, L0_attn_W_biv, L0_attn_b_biv, L0_attn_W_decay, L0_attn_b_decay, L0_attn_W_in, L0_attn_b_in, L0_ffn_router_w, L0_ffn_router_b, L0_ffn_w1, L0_ffn_b1, L0_ffn_w2, L0_ffn_b2, L1_attn_qkv_w, L1_attn_proj_w, L1_attn_proj_b, L1_ffn_ln_gamma, L1_ffn_ln_beta, L1_ffn_router_w, L1_ffn_w1, L1_ffn_w2):
    import jax
    import jax.numpy as jnp

    def _L0_tok_ref(x, proj_w, proj_b, pos_emb):
        import jax, jax.numpy as jnp
        import numpy as np
        PATCH = 16

        def _patchify(x, p):
            B, C, H, W = x.shape
            nh, nw = (H // p, W // p)
            patch_dim = C * p * p
            x = x.reshape(B, C, nh, p, nw, p)
            x = jnp.transpose(x, (0, 1, 2, 4, 3, 5))
            return x.reshape(B, -1, patch_dim)
        patches = _patchify(x, PATCH)
        out = jnp.einsum('bnp,dp->bnd', patches, proj_w) + proj_b
        return out + pos_emb

    def _L0_txt_ref(input_tensor, segment_label, token_table, segm_table):
        import jax, jax.numpy as jnp
        import numpy as np
        VOCAB = 8000
        DIM = 192
        BATCH = 8
        SEQ = 512

        def _sinusoidal_pos(seq_len, dim):
            pos = jnp.arange(seq_len, dtype=jnp.float32)[:, None]
            ids = jnp.arange(dim, dtype=jnp.float32)[None, :]
            even_exp = jnp.floor(ids / 2.0) * 2.0 / dim
            angle = pos / jnp.power(10000.0, even_exp)
            return jnp.where(jnp.arange(dim) % 2 == 0, jnp.sin(angle), jnp.cos(angle))
        batch, seq = input_tensor.shape
        pos = _sinusoidal_pos(seq, token_table.shape[1])
        tokens_embed = token_table[input_tensor]
        segments_embed = segm_table[segment_label]
        return segments_embed + pos[None, :, :] + tokens_embed

    def _L0_attn_ref(x_seq, W_biv, b_biv, W_decay, b_decay, W_in, b_in):
        import jax, jax.numpy as jnp
        import numpy as np
        B, T, D = (8, 1024, 192)
        BS = 3
        NB = D // BS

        def _rodrigues(b, v):
            theta = jnp.linalg.norm(b, axis=-1, keepdims=True)
            k = b / jnp.maximum(theta, 1e-08)
            c = jnp.cos(theta)
            s = jnp.sin(theta)
            cross = jnp.cross(k, v)
            dot = jnp.sum(k * v, axis=-1, keepdims=True)
            return v * c + cross * s + k * dot * (1.0 - c)
        Bb, Tt, Dd = x_seq.shape
        nb = Dd // BS
        biv = (jnp.einsum('btd,od->bto', x_seq, W_biv) + b_biv).reshape(Bb, Tt, nb, 3)
        decay = jax.nn.sigmoid(jnp.einsum('btd,od->bto', x_seq, W_decay) + b_decay)[..., 0]
        inj = (jnp.einsum('btd,od->bto', x_seq, W_in) + b_in).reshape(Bb, Tt, nb, 3)

        def step(h, xs):
            b_t, d_t, u_t = xs
            h_new = d_t[:, None, None] * _rodrigues(b_t, h) + u_t
            return (h_new, h_new)
        h0 = jnp.zeros((Bb, nb, 3), x_seq.dtype)
        xs = (biv.transpose(1, 0, 2, 3), decay.T, inj.transpose(1, 0, 2, 3))
        _, states = jax.lax.scan(step, h0, xs)
        return states.transpose(1, 0, 2, 3).reshape(Bb, Tt, Dd)

    def _L0_ffn_ref(x, router_w, router_b, w1, b1, w2, b2):
        import jax, jax.numpy as jnp
        import numpy as np
        EMB = 192
        HID = 288
        NUM_EXPERTS = 8
        TOP_K = 2
        B, N, E = x.shape
        T = B * N
        logits = jnp.einsum('bne,ef->bnf', x, router_w) + router_b
        probs = jax.nn.softmax(logits, axis=-1)
        topk_probs, topk_idx = jax.lax.top_k(probs, TOP_K)
        flat_x = x.reshape(T, E)
        flat_idx = topk_idx.reshape(T, TOP_K)
        flat_w = topk_probs.reshape(T, TOP_K)
        gates = jnp.zeros((T, NUM_EXPERTS), dtype=x.dtype)
        gates = gates.at[jnp.arange(T)[:, None], flat_idx].add(flat_w)
        out = jnp.zeros((T, E), dtype=x.dtype)
        for e in range(NUM_EXPERTS):
            h = jax.nn.gelu(flat_x @ w1[e] + b1[e], approximate=False)
            y = h @ w2[e] + b2[e]
            out = out + y * gates[:, e:e + 1]
        return out.reshape(B, N, E)

    def _L1_attn_ref(x, qkv_w, proj_w, proj_b):
        import jax, jax.numpy as jnp
        import numpy as np
        B, N, C = (32, 256, 192)
        H = 12
        E = C // H
        SCALE = E ** (-0.5)
        EPS = 1e-06
        b, n, c = x.shape
        qkv = jnp.einsum('bnc,dc->bnd', x, qkv_w).reshape(b, n, 3, H, E)
        q = qkv[:, :, 0]
        k = qkv[:, :, 1]
        v = qkv[:, :, 2]
        q_ = jax.nn.relu(q) + SCALE
        k_ = jax.nn.relu(k) + SCALE
        kv = jnp.einsum('bnhe,bnhd->bhed', k_, v)
        k_sum = jnp.sum(k_, axis=1)
        z = 1.0 / (jnp.einsum('bnhe,bhe->bnh', q_, k_sum) + EPS)
        out = jnp.einsum('bnhe,bhed->bnhd', q_, kv) * z[..., None]
        out = out.reshape(b, n, c)
        return jnp.einsum('bnc,dc->bnd', out, proj_w) + proj_b

    def _L1_ffn_ref(hidden_states, ln_gamma, ln_beta, router_w, w1, w2):
        import jax, jax.numpy as jnp
        import numpy as np
        D_MODEL, D_FF, N_EXPERTS, TOP_K = (192, 768, 8, 2)
        B, S = (2, 256)
        LN_EPS = 1e-05

        def _layernorm(x, gamma, beta):
            mu = jnp.mean(x, axis=-1, keepdims=True)
            var = jnp.mean(jnp.square(x - mu), axis=-1, keepdims=True)
            return (x - mu) * jax.lax.rsqrt(var + LN_EPS) * gamma + beta
        Bz, Sz, D = hidden_states.shape
        residual = hidden_states
        x = _layernorm(hidden_states, ln_gamma, ln_beta)
        tokens = x.reshape(-1, D)
        T = tokens.shape[0]
        logits = tokens @ router_w
        probs = jax.nn.softmax(logits, axis=-1)
        topw, topi = jax.lax.top_k(probs, TOP_K)
        topw = topw / jnp.sum(topw, axis=-1, keepdims=True)
        gates = jnp.zeros((T, N_EXPERTS), dtype=tokens.dtype)
        gates = gates.at[jnp.arange(T)[:, None], topi].set(topw)
        h = jnp.einsum('td,edf->etf', tokens, w1)
        h = jax.nn.silu(h)
        y = jnp.einsum('etf,efd->etd', h, w2)
        out = jnp.einsum('te,etd->td', gates, y)
        return residual + out.reshape(Bz, Sz, D)
    h = _L0_tok_ref(x, L0_tok_proj_w, L0_tok_proj_b, L0_tok_pos_emb)
    h = jnp.concatenate([h, _L0_txt_ref(x_txt, mask_BS_i2_0, L0_txt_token_table, L0_txt_segm_table)], axis=1)
    h = h + _L0_attn_ref(_layernorm(h, axis=-1), L0_attn_W_biv, L0_attn_b_biv, L0_attn_W_decay, L0_attn_b_decay, L0_attn_W_in, L0_attn_b_in)
    h = h + _L0_ffn_ref(_layernorm(h, axis=-1), L0_ffn_router_w, L0_ffn_router_b, L0_ffn_w1, L0_ffn_b1, L0_ffn_w2, L0_ffn_b2)
    h = h + _L1_attn_ref(_layernorm(h, axis=-1), L1_attn_qkv_w, L1_attn_proj_w, L1_attn_proj_b)
    h = h + _L1_ffn_ref(_layernorm(h, axis=-1), L1_ffn_ln_gamma, L1_ffn_ln_beta, L1_ffn_router_w, L1_ffn_w1, L1_ffn_w2)
    return h

_drawn_inputs = setup_inputs


def setup_inputs(seed=0):
    import zlib

    import numpy as np

    out = dict(_drawn_inputs(seed))
    spreads = {'L0_attn_b_biv': (0.0, 0.1),
     'L0_ffn_router_b': (0.0, 0.8),
     'L0_ffn_b1': (0.0, 0.8),
     'L0_ffn_b2': (0.0, 0.418),
     'L1_attn_proj_b': (0.0, 0.1),
     'L1_ffn_ln_gamma': (1.0, 0.6),
     'L1_ffn_ln_beta': (0.0, 0.8)}
    factors = {'L0_ffn_router_w': 3.155, 'L0_ffn_w1': 6.299, 'L0_ffn_w2': 5.875}
    for name, (base, spread) in spreads.items():
        noise = np.random.default_rng([zlib.crc32(name.encode()), seed]).standard_normal(out[name].shape)
        drawn = base * np.exp(spread * noise) if base else spread * noise
        out[name] = jnp.asarray(drawn.astype(out[name].dtype))
    for name, factor in factors.items():
        out[name] = (out[name] * factor).astype(out[name].dtype)
    return out
```

```python
from contextlib import ExitStack

import numpy as np

import concourse.bass as bass
from concourse import mybir

F32 = mybir.dt.float32
I32 = mybir.dt.int32
U32 = mybir.dt.uint32
ALU = mybir.AluOpType
ACT = mybir.ActivationFunctionType
AX = mybir.AxisListType.X

P = 128
B, NPATCH, NTXT, D = 8, 64, 128, 192
T = NPATCH + NTXT
NTOK = B * T
NJ = NTOK // P
NPJ = B * NPATCH // P
KC = 96
NK = D // KC
PD = 512
VOCAB, NSEG = 8000, 3
NB = D // 3
NCH = 4
NE = 8
TOPK = 2
NA = TOPK * NJ
NT = NTOK * TOPK // P + NE - 1
HID0, HID1 = 288, 768
HC0, HC1 = 96, 128
NH, HD = 12, 16
ROWS = NTOK + P
EPS = 1e-5
TCH = 64
NCHUNK = T // TCH
RING = 4

TWO_PI = 2.0 * np.pi
C1 = 6.28125
C2 = TWO_PI - C1
MAGIC = 1.5 * 2.0 ** 23
PI_DOWN = 3.1415925

C_ID, C_TRI, C_ONE, C_MASK, C_IOTA = 0, 128, 256, 384, 480
C_THR = 608
C_RST = C_THR + NJ
C_TOK = C_RST + NE * NJ
C_PAD = C_TOK + NJ
C_EPS, C_HPI, C_PART = C_PAD + 1, C_PAD + 2, C_PAD + 3
NCONST = C_PART + 1


def build(nc, x, out):
    ctx = ExitStack()
    with ctx:
        def sb(name, shape, dt=F32):
            return ctx.enter_context(nc.sbuf_tensor(name, shape, dt))

        def sem(name):
            return ctx.enter_context(nc.semaphore(name))

        class Chain:

            def __init__(self, eng, s):
                self.eng, self.sem, self.n = eng, s, 0

            def __call__(self, ins):
                self.n += 1
                ins.then_inc(self.sem, 1)
                self.eng.wait_ge(self.sem, self.n)

        xd = nc.dram_tensor("xn_rows", [ROWS, D], F32, kind="Internal").ap()
        acc = [[nc.dram_tensor(f"acc{l}_{p}", [ROWS, D], F32, kind="Internal").ap() for p in range(2)]
               for l in range(2)]

        con = sb("con", [P, NCONST])
        ident = con[:, C_ID:C_ID + P]
        iota = con[:, C_IOTA:C_IOTA + P]
        sinpos = sb("sinpos", [P, D])
        bp = sb("bp", [P, 2, D])
        h = sb("h", [P, NJ, D])
        xn = sb("xn", [P, NJ, D])
        a1 = sb("a1", [P, NJ, D])
        xT = sb("xT", [KC + 1, NK, NTOK])
        st = sb("st", [P, NJ, 6])
        mv = sb("mv", [P, NJ, 2])
        std = sb("std", [P, NJ])
        rstd = sb("rstd", [P, NJ])
        nmr = sb("nmr", [P, NJ])
        ids = sb("ids", [P, B], I32)
        ids2 = sb("ids2", [P, B], I32)
        segt = sb("segt", [NSEG, D])
        wst = sb("wst", [KC + 1, NK, 4, P])
        rw0 = sb("rw0", [KC + 1, NK, NE])
        rw1 = sb("rw1", [KC, NK, NE])
        gb = sb("gb", [KC, 2, NK])
        qkvw = sb("qkvw", [KC, NK, 3 * D])
        prw = sb("prw", [KC + 1, NK, D])
        lgs = sb("lgs", [P, NJ, NE])
        mx = sb("mx", [P, NJ, 8])
        ix = sb("ix", [P, NJ, 8], U32)
        ex = sb("ex", [P, NJ, NE + 2])
        idxf = sb("idxf", [P, NJ, 2])
        oh = sb("oh", [P, 2, NJ, NE])
        msk = sb("msk", [P, NJ, NE])
        gate = sb("gate", [P, 2, NJ])
        sm = sb("sm", [P, 3, NJ])
        rt = sb("rt", [P, 4, NE * NJ])
        te = sb("te", [P, 4, NE])
        slf = sb("slf", [P, 4, NA])
        sli = sb("sli", [P, 3, NA], I32)
        idxs = sb("idxs", [P, 32], I32)
        gs = sb("gs", [P, 32])
        etf = sb("etf", [1, 2, 32])
        et = sb("et", [1, 32], I32)
        gidx = sb("gidx", [P, RING], I32)
        sidx = sb("sidx", [P, RING], I32)
        xTs = sb("xTs", [KC + 1, 2, NK, P])

        NR1 = 23360
        reg1 = sb("reg1", [P, NR1])
        o = 0

        def carve(reg, n):
            nonlocal o
            o += n
            return reg[:, o - n:o]

        Mt = carve(reg1, T * NCH * 12).rearrange("p (t a r c) -> p t a r c", a=NCH, r=3, c=4)
        hist = carve(reg1, (T + 1) * NCH * 4).rearrange("p (t a c) -> p t a c", a=NCH, c=4)
        biv = carve(reg1, 3 * NCH * T).rearrange("p (c a t) -> p c a t", c=3, a=NCH)
        dec = carve(reg1, NCH * T).rearrange("p (a t) -> p a t", a=NCH)
        U = NCH * TCH

        def unit(n):
            v = carve(reg1, n * U)
            return v.rearrange("p (c a t) -> p c a t", c=n, a=NCH)

        sq, th, rk, yy, nn = unit(3), unit(2), unit(1), unit(1), unit(2)
        trig, kc4, dd = unit(3), unit(4), unit(3)
        sk, wk, dg, off = unit(3), unit(3), unit(3), unit(3)
        prod = carve(reg1, NCH * 12)
        assert o <= NR1
        o = 0
        w1b = carve(reg1, NE * NK * HID1)[0:KC, :].rearrange("p (e k f) -> p e k f", e=NE, k=NK)
        w2b = carve(reg1, NE * (HID1 // HC1) * D).rearrange("p (e c n) -> p e c n", e=NE, n=D)
        o = 0
        patchT = carve(reg1, 4 * PD).rearrange("p (k t) -> p k t", k=4)
        projT = carve(reg1, 4 * D).rearrange("p (k n) -> p k n", k=4)
        lab = carve(reg1, B * NTXT)[0:NSEG, :].bitcast(I32)
        lab2 = carve(reg1, B * NTXT)[0:NSEG, :].bitcast(I32)
        lab3 = carve(reg1, B * NTXT)[0:NSEG, :].bitcast(I32)
        ohl = carve(reg1, B * NTXT)[0:NSEG, :]
        zero = carve(reg1, (ROWS // P) * D)

        NR2 = NE * NK * HID0 + NE * (HID0 // HC0) * D
        reg2 = sb("reg2", [P, NR2])
        o = 0
        w1a = carve(reg2, NE * NK * HID0)[0:KC + 1, :].rearrange("p (e k f) -> p e k f", e=NE, k=NK)
        w2a = carve(reg2, NE * (HID0 // HC0) * D)[0:KC + 1, :].rearrange("p (e c n) -> p e c n", e=NE, n=D)
        o = 0
        qT = carve(reg2, NK * NTOK)[0:KC, :].rearrange("p (g t) -> p g t", g=NK)
        kb = carve(reg2, NJ * D).rearrange("p (j n) -> p j n", j=NJ)
        vb = carve(reg2, NJ * NK * (KC + 1)).rearrange("p (j g n) -> p j g n", j=NJ, g=NK)
        kvm = carve(reg2, 2 * NK * KC)[0:KC, :].rearrange("p (i g n) -> p i g n", i=2, g=NK)
        ksm = carve(reg2, 2 * NK * KC)[0:KC, :].rearrange("p (i g n) -> p i g n", i=2, g=NK)
        rec = carve(reg2, NK * T)[0:KC, :].rearrange("p (g t) -> p g t", g=NK)
        assert o <= NR2

        reg3 = sb("reg3", [P, NA * P])
        oneA = reg3[:, :].rearrange("p (a r) -> p a r", a=NA)
        oneB = a1[:, :, :].rearrange("p j n -> p (j n)")[:, 0:NA * 64].rearrange("p (a v q) -> p a v q", a=NA, v=2)
        attT = reg3[0:KC + 1, 0:NK * NTOK].rearrange("p (g b t) -> p g b t", g=NK, b=B)
        o = 0
        hact = carve(reg3, HID1)
        hTs = carve(reg3, HID1)
        xs = carve(reg3, RING * D).rearrange("p (s n) -> p s n", s=RING)
        ys = carve(reg3, RING * D).rearrange("p (s n) -> p s n", s=RING)

        bank = [ctx.enter_context(nc.psum_tensor(f"bank{i}", [P, 512], F32)) for i in range(8)]

        ld_con = sem("ld_con"); ld_lab = sem("ld_lab"); ld_ids = sem("ld_ids"); ld_seg = sem("ld_seg")
        ld_patch = sem("ld_patch"); ld_pos = sem("ld_pos"); ld_wst = sem("ld_wst")
        ld_ffn0 = sem("ld_ffn0"); ld_attn = sem("ld_attn"); ld_ffn1 = sem("ld_ffn1"); ld_rt = sem("ld_rt")
        zero_ready = sem("zero_ready"); zero_done = sem("zero_done"); bzero_done = sem("bzero_done")
        ids_ready = sem("ids_ready"); ohl_ready = sem("ohl_ready")
        gath = [sem(f"gath{q}") for q in range(4)]
        patch_mm = sem("patch_mm"); seg_mm = sem("seg_mm")
        ones_ready = sem("ones_ready")
        dve_self = sem("dve_self"); act_self = sem("act_self"); pool_self = sem("pool_self"); pool_turn = sem("pool_turn")
        scan_self = sem("scan_self")
        var_ready = sem("var_ready"); std_ready = sem("std_ready"); rstd_ready = sem("rstd_ready")
        xn_ready = sem("xn_ready"); xt_psum = sem("xt_psum"); xT_ready = sem("xT_ready")
        h_ready = sem("h_ready")
        proj_mm = sem("proj_mm"); ev_act = sem("ev_act"); ev_dve = sem("ev_dve")
        sq_ready = sem("sq_ready"); th2_ready = sem("th2_ready"); th_ready = sem("th_ready")
        rk_ready = sem("rk_ready"); y_ready = sem("y_ready"); trig_ready = sem("trig_ready")
        m_ready = sem("m_ready")
        scanned = sem("scanned"); back_mm = sem("back_mm")
        xd_written = sem("xd_written")
        lg_mm = sem("lg_mm"); ex_in = sem("ex_in"); ex_out = sem("ex_out"); msk_ready = sem("msk_ready")
        rank_mm = sem("rank_mm"); one_ready = sem("one_ready"); inv_mm = sem("inv_mm")
        route_done = sem("route_done")
        gidx_ready = sem("gidx_ready"); sidx_ready = sem("sidx_ready")
        xs_ready = [sem(f"xs_ready{s}") for s in range(RING)]
        scat = [sem(f"scat{s}") for s in range(RING)]
        tx_mm = sem("tx_mm"); tx_ev = sem("tx_ev"); g1_mm = sem("g1_mm"); act_done = sem("act_done")
        th_mm = sem("th_mm"); th_ev = sem("th_ev"); g2_mm = sem("g2_mm"); y_ev = sem("y_ev")
        acc_ld = [sem(f"acc_ld{g}") for g in range(2)]
        kv_mm = sem("kv_mm"); kv_ev = sem("kv_ev"); q_mm = sem("q_mm"); q_ev = sem("q_ev")
        st_mm = sem("st_mm"); st_ev = sem("st_ev"); nd_mm = sem("nd_mm"); att_ready = sem("att_ready")
        pr_mm = sem("pr_mm"); fin_ready = sem("fin_ready"); stored = sem("stored")

        block = ctx.enter_context(nc.Block())

        NPAIR = NJ // 2
        XT_PASS = {1: 0, 2: 1, 3: 2, 5: 3}

        def tok_rows(dram, buf, eng, s):
            dv = dram[0:NTOK, :].rearrange("(b t) n -> b t n", b=B)
            pairs = [(dv[b, 0:NPATCH, :], buf[NPATCH * (b % 2):NPATCH * (b % 2) + NPATCH, b // 2, :])
                     for b in range(B)]
            pairs.append((dv[:, NPATCH:T, :].rearrange("b t n -> t b n"), buf[:, NPJ:NJ, :]))
            return pairs

        def prep_angle(eng, ns, link, c):
            tt, ts = ns.tensor_tensor, ns.tensor_scalar
            eng.wait_ge(sq_ready, c + 1)
            link(tt(th[:, 0], sq[:, 0], sq[:, 1], ALU.add))
            tt(th[:, 0], th[:, 0], sq[:, 2], ALU.add).then_inc(th2_ready, 1)
            eng.wait_ge(th_ready, c + 1)
            link(ts(yy[:, 0], th[:, 1], float(1.0 / TWO_PI), MAGIC, ALU.mult, ALU.add))
            ts(nn[:, 0], yy[:, 0], MAGIC, -C1, ALU.subtract, ALU.mult)
            link(ts(nn[:, 1], yy[:, 0], MAGIC, -C2, ALU.subtract, ALU.mult))
            link(tt(nn[:, 0], nn[:, 0], th[:, 1], ALU.add))
            link(tt(yy[:, 0], nn[:, 0], nn[:, 1], ALU.add))
            ts(yy[:, 0], yy[:, 0], -PI_DOWN, PI_DOWN, ALU.max, ALU.min).then_inc(y_ready, 1)

        def prep_matrix(eng, ns, link, c):
            tt = ns.tensor_tensor
            t0 = c * TCH
            b3 = [P, 3, NCH, TCH]
            eng.wait_ge(rk_ready, c + 1)
            tt(kc4[:, 0:3], biv[:, :, :, t0:t0 + TCH], rk[:, 0:1].to_broadcast(b3), ALU.mult)
            link(tt(kc4[:, 3], biv[:, 0, :, t0:t0 + TCH], rk[:, 0], ALU.mult))
            eng.wait_ge(trig_ready, c + 1)
            d = dec[:, :, t0:t0 + TCH]
            tt(dd[:, 0], trig[:, 0], d, ALU.mult)
            link(tt(dd[:, 1], trig[:, 2], d, ALU.mult))
            link(tt(dd[:, 2], d, dd[:, 1], ALU.subtract))
            tt(sk, kc4[:, 0:3], dd[:, 0:1].to_broadcast(b3), ALU.mult)
            link(tt(wk, kc4[:, 0:3], dd[:, 2:3].to_broadcast(b3), ALU.mult))
            tt(dg, wk, kc4[:, 0:3], ALU.mult)
            link(tt(off, wk, kc4[:, 1:4], ALU.mult))

            def ent(r, cc):
                return Mt[:, t0:t0 + TCH, :, r, cc].rearrange("p t a -> p a t")

            for r in range(3):
                tt(ent(r, r), dg[:, r], dd[:, 1], ALU.add)
            last = None
            for r in range(3):
                q, s = (r + 1) % 3, (r + 2) % 3
                tt(ent(r, q), off[:, r], sk[:, s], ALU.subtract)
                last = tt(ent(q, r), off[:, r], sk[:, s], ALU.add)
            link(last)
            eng.sem_inc(m_ready, 1)

        def trig_of(act, link, c):
            t0 = c * TCH
            act.wait_ge(ev_dve, 3 if c == 0 else 9)
            nc.scalar.activation(sq, biv[:, :, :, t0:t0 + TCH], ACT.Square).then_inc(sq_ready, 1)
            act.wait_ge(th2_ready, c + 1)
            nc.scalar.activation(th[:, 1], th[:, 0], ACT.Sqrt).then_inc(th_ready, 1)
            act.wait_ge(y_ready, c + 1)
            nc.scalar.activation(trig[:, 0], yy[:, 0], ACT.Sin)
            link(nc.scalar.activation(trig[:, 1], yy[:, 0], ACT.Abs))
            nc.scalar.activation(trig[:, 2], trig[:, 1], ACT.Sin, bias=con[:, C_HPI:C_HPI + 1],
                                 scale=-1.0).then_inc(trig_ready, 1)

        def recip_of(dve, V, link, c):
            dve.wait_ge(th_ready, c + 1)
            link(V.tensor_scalar(rk[:, 0], th[:, 1], 1e-8, None, ALU.max))
            V.reciprocal(rk[:, 0], rk[:, 0]).then_inc(rk_ready, 1)

        @block.sync
        def _(sp):
            sp.dma_start(con[:, :], x["consts"]).then_inc(ld_con, 16)
            sp.dma_start(patchT, x["patchT"].rearrange("(k p) t -> p k t", p=P)).then_inc(ld_patch, 16)
            sp.dma_start(projT, x["projT"].rearrange("(k p) n -> p k n", p=P)).then_inc(ld_patch, 16)
            for k in range(NK):
                sp.dma_start(wst[0:KC, k, :, :], x["wst"][k * KC:(k + 1) * KC, :, :]).then_inc(ld_wst, 16)
            sp.dma_start(wst[KC:KC + 1, 1, :, :], x["wst_b"]).then_inc(ld_wst, 16)
            sp.wait_ge(zero_ready, 1)
            for l in range(2):
                for p in range(2):
                    sp.dma_start(acc[l][p].rearrange("(a p) n -> p a n", p=P),
                                 zero.rearrange("p (a n) -> p a n", n=D)).then_inc(zero_done, 16)
            sp.dma_start(xd[NTOK:ROWS, :], zero[:, 0:D]).then_inc(zero_done, 16)
            for e in range(NE):
                sp.dma_start(w1a[0:KC, e, :, :], x["w1a"][e].rearrange("(k p) f -> p k f", p=KC)).then_inc(ld_ffn0, 16)
                sp.dma_start(w2a[0:KC, e, :, :], x["w2a"][e].rearrange("(c p) n -> p c n", p=KC)).then_inc(ld_ffn0, 16)
            sp.dma_start(w1a[KC:KC + 1, :, 1, :], x["b1a"].rearrange("(a e) f -> a e f", a=1)).then_inc(ld_ffn0, 16)
            sp.dma_start(w2a[KC:KC + 1, :, 2, :], x["b2a"].rearrange("(a e) n -> a e n", a=1)).then_inc(ld_ffn0, 16)

            def write_rows(n):
                for dst, src in tok_rows(xd, xn, sp, None):
                    sp.dma_start(dst, src).then_inc(xd_written, 16)

            def load_acc(l):
                for s in range(RING):
                    sp.wait_ge(scat[s], 16 * (sum(1 for i in range(NT) if i % RING == s) * (l + 1)))
                for p, buf in enumerate((xn, a1)):
                    for dr, sbuf in tok_rows(acc[l][p], buf, sp, None):
                        sp.dma_start(sbuf, dr).then_inc(acc_ld[p], 16)

            sp.wait_ge(xn_ready, 2 * NJ)
            write_rows(0)
            sp.wait_ge(h_ready, 2)
            for e in range(NE):
                sp.dma_start(w1b[:, e, :, :], x["w1b"][e].rearrange("(k p) f -> p k f", p=KC)).then_inc(ld_ffn1, 16)
                sp.dma_start(w2b[:, e, :, :], x["w2b"][e].rearrange("(c p) n -> p c n", p=HC1)).then_inc(ld_ffn1, 16)
            load_acc(0)
            sp.wait_ge(xn_ready, 5 * NJ)
            write_rows(1)
            load_acc(1)
            sp.wait_ge(fin_ready, 1)
            for dr, sbuf in tok_rows(out, h, sp, None):
                sp.dma_start(dr, sbuf).then_inc(stored, 16)
            sp.wait_ge(stored, 16 * 9)

        @block.gpsimd
        def _(pool):
            link = Chain(pool, pool_self)
            nc.gpsimd.memset(zero, 0.0).then_inc(zero_ready, 1)
            pool.wait_ge(ids_ready, 1)
            for b in range(B):
                pool.indirect_dma_start(xn[:, NPJ + b, :], None, x["table"],
                                        bass.IndirectOffsetOnAxis(ap=ids2[:, b:b + 1], axis=0)
                                        ).then_inc(gath[b // 2], 16)

            for c in range(1, NCHUNK):
                prep_angle(pool, nc.gpsimd, link, c)
                prep_matrix(pool, nc.gpsimd, link, c)

            def expert_dma(l):
                base = {s: l * sum(1 for i in range(NT) if i % RING == s) for s in range(RING)}

                def gather(iv, s, pro=False):
                    pool.wait_ge(gidx_ready, l * NT + iv * RING + s + 1)
                    if pro:
                        if l:
                            pool.wait_ge(tx_mm, l * NT)
                    else:
                        pool.wait_ge(tx_mm, l * NT + (iv - 1) * RING + s + 1)
                    pool.sem_inc(pool_turn, 1)
                    pool.indirect_dma_start(xs[:, s, :], None, xd,
                                            bass.IndirectOffsetOnAxis(ap=gidx[:, s:s + 1], axis=0)
                                            ).then_inc(xs_ready[s], 16)

                def scatter(iv, s):
                    i = iv * RING + s
                    pool.wait_ge(sidx_ready, l * NT + i + 1)
                    pool.wait_ge(y_ev, l * NT + i + 1)
                    s2 = (s - 2) % RING
                    n = base[s2] + iv + (1 if s >= 2 else 0)
                    if not (isinstance(n, int) and n == 0):
                        pool.wait_ge(scat[s2], 16 * n)
                    pool.sem_inc(pool_turn, 1)
                    pool.indirect_dma_start(acc[l][s % 2],
                                            bass.IndirectOffsetOnAxis(ap=sidx[:, s:s + 1], axis=0),
                                            ys[:, s, :], None, compute_op=ALU.add).then_inc(scat[s], 16)

                pool.wait_ge(xd_written, 16 * 9 * (l + 1))
                pool.wait_ge(zero_done, 16 * 5)
                for s in range(RING):
                    gather(0, s, pro=True)
                for s in range(RING):
                    gather(1, s)
                    scatter(0, s)
                with pool.Fori(1, NT // RING - 1) as iv:
                    for s in range(RING):
                        gather(iv + 1, s)
                        scatter(iv, s)
                last = NT // RING - 1
                for s in range(RING):
                    if (last + 1) * RING + s < NT:
                        gather(last + 1, s)
                    scatter(last, s)
                for s in range(NT - (last + 1) * RING):
                    scatter(last + 1, s)

            for l in range(2):
                expert_dma(l)

        @block.scalar
        def _(act):
            link = Chain(act, act_self)
            act.dma_start(lab, x["labels"].partition_broadcast(NSEG)).then_inc(ld_lab, 16)
            act.dma_start(ids[:, :], x["ids"]).then_inc(ld_ids, 16)
            act.dma_start(segt[:, :], x["segm"]).then_inc(ld_seg, 16)
            act.dma_start(sinpos[:, :], x["sinpos"]).then_inc(ld_pos, 16)
            act.dma_start(bp[0:NPATCH, 0, :], x["pos"]).then_inc(ld_pos, 16)
            act.dma_start(bp[NPATCH:P, 0, :], x["pos"]).then_inc(ld_pos, 16)
            act.dma_start(bp[:, 1, :], x["projb"].partition_broadcast(P)).then_inc(ld_pos, 16)
            for k in range(NK):
                rows = slice(k * KC, (k + 1) * KC)
                act.dma_start(rw0[0:KC, k, :], x["rw0"][rows, :]).then_inc(ld_rt, 16)
                act.dma_start(rw1[:, k, :], x["rw1"][rows, :]).then_inc(ld_rt, 16)
                act.dma_start(qkvw[:, k, :], x["qkvT"][rows, :]).then_inc(ld_attn, 16)
                act.dma_start(prw[0:KC, k, :], x["prT"][rows, :]).then_inc(ld_attn, 16)
            act.dma_start(rw0[KC:KC + 1, 1, :], x["rb0"]).then_inc(ld_rt, 16)
            act.dma_start(gb[:, :, :], x["gb"]).then_inc(ld_rt, 16)
            act.dma_start(prw[KC:KC + 1, 1, :], x["prb"]).then_inc(ld_attn, 16)

            act.wait_ge(ld_con, 16)

            def ln(n, src, dst):
                for g in range(3):
                    js = slice(4 * g, 4 * g + 4)
                    act.wait_ge(var_ready, 3 * (n - 1) + g + 1)
                    nc.scalar.activation(std[:, js], mv[:, js, 1], ACT.Sqrt,
                                         bias=con[:, C_EPS:C_EPS + 1]).then_inc(std_ready, 1)
                for g in range(3):
                    act.wait_ge(rstd_ready, 3 * (n - 1) + g + 1)
                    for j in range(4 * g, 4 * g + 4):
                        nc.scalar.activation(dst[:, j, :], src[:, j, :], ACT.Identity,
                                             bias=nmr[:, j:j + 1], scale=rstd[:, j:j + 1]).then_inc(xn_ready, 1)

            ln(1, h, xn)

            act.wait_ge(zero_done, 16 * 5)
            for g in range(3):
                for cc in range(4):
                    u = 4 * g + cc
                    act.wait_ge(proj_mm, u + 1)
                    ps = bank[2 + u % 6]
                    if g == 0:
                        halves = [(0, 0, 0, NPATCH), (1, 256, 0, NPATCH)]
                    else:
                        halves = [(g - 1, 0, NPATCH, T)]
                    for k, (hf, col, t0, t1) in enumerate(halves):
                        n = NCH * (t1 - t0)
                        pr = slice(64 * hf, 64 * hf + 64)
                        if cc == 0:
                            ins = nc.scalar.activation(
                                dec[pr, :, t0:t1], ps[pr, col:col + n].rearrange("p (a t) -> p a t", a=NCH),
                                ACT.Sigmoid)
                        else:
                            ins = nc.scalar.activation(
                                Mt[pr, t0:t1, :, cc - 1, 3].rearrange("p t a -> p a t"),
                                ps[64:128, col:col + n].rearrange("p (a t) -> p a t", a=NCH), ACT.Copy)
                    ins.then_inc(ev_act, 1)
                if g == 0:
                    trig_of(act, link, 0)
            for c in range(1, NCHUNK):
                act.wait_ge(m_ready, c)
                trig_of(act, link, c)

            def experts(l, func, hid):
                def copy_g(iv, s, first=False):
                    if not first:
                        act.wait_ge(xs_ready[s], 16 * (per[s] * l + iv))
                    nc.scalar.activation(gidx[:, s:s + 1], idxs[:, bass.ds(iv * RING + s, 1)],
                                         ACT.Copy).then_inc(gidx_ready, 1)

                def copy_s(iv, s, first=False):
                    if not first:
                        act.wait_ge(scat[s], 16 * (per[s] * l + iv))
                    nc.scalar.activation(sidx[:, s:s + 1], idxs[:, bass.ds(iv * RING + s, 1)],
                                         ACT.Copy).then_inc(sidx_ready, 1)

                def nonlin(i):
                    act.wait_ge(g1_mm, l * NT + i + 1)
                    if not (isinstance(i, int) and i == 0 and l == 0):
                        act.wait_ge(th_mm, l * NT + i)
                    if hid == HID0:
                        nc.scalar.activation(hact[:, 0:hid], bank[2][:, 0:hid], func).then_inc(act_done, 1)
                    else:
                        half = hid // 2
                        nc.scalar.activation(hact[:, 0:half], bank[2][:, 0:half], func)
                        nc.scalar.activation(hact[:, half:hid], bank[3][:, 0:half], func).then_inc(act_done, 1)

                per = [sum(1 for i in range(NT) if i % RING == s) for s in range(RING)]
                act.wait_ge(route_done, l + 1)
                if l:
                    for s in range(RING):
                        act.wait_ge(scat[s], 16 * per[s])
                for s in range(RING):
                    copy_g(0, s, first=True)
                nonlin(0)

                def step(iv, s, first=False, g=True, more=True):
                    if g:
                        copy_g(iv + 1, s)
                    copy_s(iv, s, first=first)
                    if more:
                        nonlin(iv * RING + s + 1)

                for s in range(RING):
                    step(0, s, first=True)
                last = NT // RING - 1
                with act.Fori(1, last) as iv:
                    for s in range(RING):
                        step(iv, s)
                for s in range(RING):
                    step(last, s, g=(last + 1) * RING + s < NT)
                for s in range(NT - (last + 1) * RING):
                    step(last + 1, s, g=False, more=(last + 1) * RING + s + 1 < NT)

            ln(2, h, xn)
            act.wait_ge(ex_in, 1)
            nc.scalar.activation(ex[:, :, :], ex[:, :, :], ACT.Exp).then_inc(ex_out, 1)
            experts(0, ACT.Gelu, HID0)

            ln(3, h, xn)

            ln(4, h, xn)
            ln(5, xn, xn)
            act.wait_ge(ex_in, 2)
            nc.scalar.activation(ex[:, :, :], ex[:, :, :], ACT.Exp).then_inc(ex_out, 1)
            experts(1, ACT.Silu, HID1)

        @block.vector
        def _(dve):
            link = Chain(dve, dve_self)
            V = nc.vector
            V.memset(xT[KC:KC + 1, 1, :], 1.0)
            V.memset(xTs[KC:KC + 1, :, 1, :], 1.0).then_inc(ones_ready, 1)

            dve.wait_ge(ld_lab, 16)
            dve.wait_ge(ld_con, 16)
            link(V.tensor_scalar(lab2, lab, 0, NSEG, ALU.is_lt, ALU.mult))
            link(V.tensor_tensor(lab3, lab, lab2, ALU.add))
            link(V.tensor_scalar(lab2, lab3, 0, NSEG - 1, ALU.max, ALU.min))
            V.tensor_scalar(ohl, lab2, con[0:NSEG, C_PART:C_PART + 1], None, ALU.is_equal).then_inc(ohl_ready, 1)
            dve.wait_ge(ld_ids, 16)
            link(V.tensor_scalar(ids2[:, :], ids[:, :], 0, VOCAB, ALU.is_lt, ALU.mult))
            link(V.tensor_tensor(ids2[:, :], ids[:, :], ids2[:, :], ALU.add))
            V.tensor_scalar(ids2[:, :], ids2[:, :], 0, VOCAB - 1, ALU.max, ALU.min).then_inc(ids_ready, 1)
            dve.wait_ge(ld_pos, 64)
            link(V.tensor_tensor(bp[:, 0, :], bp[:, 0, :], bp[:, 1, :], ALU.add))
            for q in range(2):
                dve.wait_ge(patch_mm, q + 1)
                last = V.tensor_tensor(h[:, 2 * q:2 * q + 2, :],
                                       bank[q][:, 0:2 * D].rearrange("p (a n) -> p a n", a=2),
                                       bp[:, 0:1, :].to_broadcast([P, 2, D]), ALU.add)
            for q in range(4):
                dve.wait_ge(seg_mm, q + 1)
                last = V.tensor_tensor(h[:, NPJ + 2 * q:NPJ + 2 * q + 2, :],
                                       bank[2 + q][:, 0:2 * D].rearrange("p (a n) -> p a n", a=2),
                                       sinpos[:, :].unsqueeze(1).to_broadcast([P, 2, D]), ALU.add)
            link(last)
            for q in range(4):
                dve.wait_ge(gath[q], 32)
                js = slice(NPJ + 2 * q, NPJ + 2 * q + 2)
                last = V.tensor_tensor(h[:, js, :], h[:, js, :], xn[:, js, :], ALU.add)
            link(last)

            def ln_start(src, g):
                for j in range(4 * g, 4 * g + 4):
                    last = V.bn_stats(st[:, j, :], src[:, j, :])
                link(last)
                for j in range(4 * g, 4 * g + 4):
                    last = V.bn_aggr(mv[:, j, :], st[:, j, :])
                last.then_inc(var_ready, 1)

            def ln_end(n, g):
                js = slice(4 * g, 4 * g + 4)
                dve.wait_ge(std_ready, 3 * (n - 1) + g + 1)
                link(V.reciprocal(rstd[:, js], std[:, js]))
                V.scalar_tensor_tensor(out=nmr[:, js], in0=mv[:, js, 0], scalar=-1.0, in1=rstd[:, js],
                                       op0=ALU.mult, op1=ALU.mult).then_inc(rstd_ready, 1)

            def ln(n, src):
                for g in range(3):
                    ln_start(src, g)
                    if g:
                        ln_end(n, g - 1)
                ln_end(n, 2)

            def xt_evac(n):
                m = XT_PASS[n]
                for q in range(NPAIR):
                    dve.wait_ge(xt_psum, m * NPAIR + q + 1)
                    src = bank[q % 2][0:KC, :].rearrange("p (k t) -> p k t", k=NK)
                    dst = xT[0:KC, :, 256 * q:256 * q + 256]
                    if n == 5:
                        for k in range(NK):
                            last = V.tensor_scalar(dst[:, k, :], src[:, k, :], gb[:, 0, k:k + 1], gb[:, 1, k:k + 1],
                                                   ALU.mult, ALU.add)
                        last.then_inc(xT_ready, 1)
                    else:
                        V.tensor_copy(dst, src).then_inc(xT_ready, 1)

            ln(1, h)
            xt_evac(1)
            dve.wait_ge(zero_done, 16 * 5)
            V.memset(hist, 1.0)
            link(V.memset(prod, 0.0))
            link(V.memset(hist[:, 0, :, 0:3], 0.0))

            for g in range(3):
                for c in range(3):
                    u = 4 * g + c + 1
                    dve.wait_ge(proj_mm, u + 1)
                    ps = bank[2 + u % 6]
                    if g == 0:
                        halves = [(0, 0, 0, NPATCH), (1, 256, 0, NPATCH)]
                    else:
                        halves = [(g - 1, 0, NPATCH, T)]
                    for hf, col, t0, t1 in halves:
                        n = NCH * (t1 - t0)
                        ins = V.tensor_copy(biv[64 * hf:64 * hf + 64, c, :, t0:t1],
                                            ps[0:64, col:col + n].rearrange("p (a t) -> p a t", a=NCH))
                    ins.then_inc(ev_dve, 1)
                if g == 0:
                    prep_angle(dve, V, link, 0)
                    recip_of(dve, V, link, 0)

            dve.wait_ge(ev_act, 4)
            prep_matrix(dve, V, link, 0)

            def steps(t0, n):
                def one(t, k):
                    if not (isinstance(k, int) and k == 0):
                        dve.wait_ge(scan_self, k)
                    V.tensor_tensor(prod.rearrange("p (a r c) -> p a r c", a=NCH, r=3),
                                    Mt[:, bass.ds(t, 1)].rearrange("p o a r c -> p (o a) r c"),
                                    hist[:, bass.ds(t, 1)].rearrange("p o a c -> p a o c")
                                    .to_broadcast([P, NCH, 3, 4]), ALU.mult).then_inc(scan_self, 1)
                    dve.wait_ge(scan_self, k + 1)
                    V.tensor_reduce(hist[:, bass.ds(t + 1, 1), :, 0:3].rearrange("p o a c -> p (o a) c"),
                                    prod.rearrange("p (a r c) -> p a r c", a=NCH, r=3),
                                    AX, ALU.add).then_inc(scan_self, 1)

                if t0 == 0:
                    for u in range(16):
                        one(u, 2 * u)
                    t0, n = 16, n - 16
                with dve.Fori(0, n // 16) as i:
                    for u in range(16):
                        one(i * 16 + (t0 + u), i * 32 + 2 * (t0 + u))

            for c in range(NCHUNK):
                if c:
                    dve.wait_ge(m_ready, c + 1)
                    dve.wait_ge(ev_act, 12)
                steps(c * TCH, TCH // 2)
                if c + 1 < NCHUNK:
                    recip_of(dve, V, link, c + 1)
                steps(c * TCH + TCH // 2, TCH // 2)
            dve.wait_ge(scan_self, 2 * T)
            dve.sem_inc(scanned, 1)

            for q in range(2):
                dve.wait_ge(back_mm, q + 1)
                hv = h[:, q:q + 3:2, :].rearrange("p a (n c) -> p a c n", c=3)
                last = V.tensor_tensor(hv, hv, bank[q][:, 0:384].rearrange("p (c a n) -> p a c n", c=3, a=2), ALU.add)
            for ch in range(NCH):
                dve.wait_ge(back_mm, 3 + ch)
                hv = h[:, NPJ + ch:NPJ + ch + 5:4, :].rearrange("p a (n c) -> p a c n", c=3)
                last = V.tensor_tensor(hv, hv, bank[2 + ch][:, 0:384].rearrange("p (c a n) -> p a c n", c=3, a=2),
                                       ALU.add)
            link(last)
            dve.sem_inc(h_ready, 2)

            def route(l):
                b12, b8 = [P, NJ, NE], [P, NE, NJ]
                dve.wait_ge(lg_mm, l + 1)
                link(V.tensor_copy(lgs[:, :, :], bank[7][:, 0:NJ * NE].rearrange("p (j e) -> p j e", j=NJ)))
                for j in range(NJ):
                    last = V.max(mx[:, j, :], lgs[:, j, :])
                link(last)
                for j in range(NJ):
                    last = V.max_index(ix[:, j, :], mx[:, j, :], lgs[:, j, :])
                link(last)
                m0 = mx[:, :, 0:1]
                V.tensor_tensor(ex[:, :, 0:NE], lgs[:, :, :], m0.to_broadcast(b12), ALU.subtract)
                V.tensor_tensor(ex[:, :, NE:NE + 2], mx[:, :, 0:2], m0.to_broadcast([P, NJ, 2]),
                                ALU.subtract).then_inc(ex_in, 1)
                link(V.tensor_copy(idxf[:, :, :], ix[:, :, 0:2]))
                for k in range(2):
                    last = V.tensor_tensor(oh[:, k], iota[:, 0:NE].unsqueeze(1).to_broadcast(b12),
                                           idxf[:, :, k:k + 1].to_broadcast(b12), ALU.is_equal)
                link(last)
                V.tensor_tensor(msk[:, :, :], oh[:, 0], oh[:, 1], ALU.add).then_inc(msk_ready, 1)
                dve.wait_ge(ex_out, l + 1)
                link(V.tensor_reduce(sm[:, 0, :], ex[:, :, 0:NE], AX, ALU.add))
                link(V.reciprocal(sm[:, 1, :], sm[:, 0, :]))
                link(V.tensor_tensor(gate[:, :, :], ex[:, :, NE:NE + 2].rearrange("p j k -> p k j"),
                                     sm[:, 1:2, :].to_broadcast([P, 2, NJ]), ALU.mult))
                if l == 1:
                    link(V.tensor_tensor(sm[:, 0, :], gate[:, 0, :], gate[:, 1, :], ALU.add))
                    link(V.reciprocal(sm[:, 1, :], sm[:, 0, :]))
                    link(V.tensor_tensor(gate[:, :, :], gate[:, :, :],
                                         sm[:, 1:2, :].to_broadcast([P, 2, NJ]), ALU.mult))
                tot, cum, rs = rt[:, 0, :], rt[:, 1, :], con[:, C_RST:C_RST + NE * NJ]
                totv = tot.rearrange("p (e j) -> p e j", e=NE)
                cumv = cum.rearrange("p (e j) -> p e j", e=NE)
                dve.wait_ge(rank_mm, l + 1)
                link(V.tensor_copy(totv, bank[7][:, 192:288].rearrange("p (j e) -> p e j", j=NJ)))
                link(V.tensor_tensor_scan(cum, rs, tot, 0.0, ALU.mult, ALU.add))
                cmpv = rt[:, 2, :].rearrange("p (e j) -> p e j", e=NE)
                link(V.tensor_tensor(cmpv, cumv[:, :, NJ - 1:NJ].to_broadcast(b8),
                                     con[:, C_THR:C_THR + NJ].unsqueeze(1).to_broadcast(b8), ALU.is_gt))
                link(V.tensor_reduce(te[:, 0, :], cmpv, AX, ALU.add))
                link(V.tensor_tensor_scan(te[:, 1, :], con[:, C_ONE:C_ONE + NE], te[:, 0, :], 0.0, ALU.mult, ALU.add))
                link(V.tensor_tensor(te[:, 2, :], te[:, 1, :], te[:, 0, :], ALU.subtract))
                link(V.tensor_scalar(te[:, 3, :], te[:, 2, :], float(P), None, ALU.mult))
                link(V.tensor_tensor(cumv, cumv, totv, ALU.subtract))
                link(V.tensor_tensor(cumv, cumv, te[:, 3, :].unsqueeze(2).to_broadcast(b8), ALU.add))
                slv = rt[:, 2, :].rearrange("p (j e) -> p j e", j=NJ)
                link(V.tensor_tensor(slv, bank[7][:, 96:192].rearrange("p (j e) -> p j e", j=NJ),
                                     cumv.rearrange("p e j -> p j e"), ALU.add))
                for k in range(2):
                    link(V.tensor_tensor(rt[:, 3, :].rearrange("p (j e) -> p j e", j=NJ), oh[:, k], slv, ALU.mult))
                    link(V.tensor_reduce(slf[:, 0, k * NJ:(k + 1) * NJ],
                                         rt[:, 3, :].rearrange("p (j e) -> p j e", j=NJ), AX, ALU.add))
                link(V.tensor_copy(sli[:, 0, :], slf[:, 0, :]))
                V.tensor_scalar(sli[:, 1, :], sli[:, 0, :], 7, None, ALU.arith_shift_right)
                link(V.tensor_scalar(sli[:, 2, :], sli[:, 0, :], P - 1, None, ALU.bitwise_and))
                link(V.tensor_copy(slf[:, 1:3, :], sli[:, 1:3, :]))
                bq = [P, NA, 32]
                link(V.tensor_tensor(oneA[:, :, 0:32], iota[:, 0:32].unsqueeze(1).to_broadcast(bq),
                                     slf[:, 1, :].unsqueeze(2).to_broadcast(bq), ALU.is_equal))
                for k in range(2):
                    ks = slice(k * NJ, (k + 1) * NJ)
                    bk = [P, NJ, 32]
                    V.tensor_tensor(oneB[:, ks, 0, :], oneA[:, ks, 0:32],
                                    con[:, C_TOK:C_TOK + NJ].unsqueeze(2).to_broadcast(bk), ALU.mult)
                    last = V.tensor_tensor(oneB[:, ks, 1, :], oneA[:, ks, 0:32],
                                           gate[:, k, :].unsqueeze(2).to_broadcast(bk), ALU.mult)
                link(last)
                for k in range(4):
                    ks = slice(k * NA // 4, (k + 1) * NA // 4)
                    ba = [P, NA // 4, P]
                    V.tensor_tensor(oneA[:, ks, :], iota.unsqueeze(1).to_broadcast(ba),
                                    slf[:, 2, ks].unsqueeze(2).to_broadcast(ba), ALU.is_equal).then_inc(one_ready, 1)
                be = [1, 32, NE]
                ev = rt[0:1, 0:3, :].rearrange("p a n -> p (a n)")[:, 0:32 * NE].rearrange("p (i e) -> p i e", e=NE)
                link(V.tensor_tensor(ev, iota[0:1, 0:32].unsqueeze(2).to_broadcast(be),
                                     te[0:1, 1, :].unsqueeze(1).to_broadcast(be), ALU.is_ge))
                link(V.tensor_reduce(etf[:, 0, :], ev, AX, ALU.add))
                link(V.tensor_scalar(etf[:, 1, :], etf[:, 0, :], float(NE - 1), None, ALU.min))
                link(V.tensor_copy(et[:, :], etf[:, 1, :]))
                dve.wait_ge(inv_mm, l + 1)
                link(V.tensor_scalar(rt[:, 0, 0:32], bank[6][:, 0:32], 0.0, con[:, C_PAD:C_PAD + 1],
                                     ALU.is_equal, ALU.mult))
                V.tensor_copy(gs[:, :], bank[6][:, 32:64])
                link(V.scalar_tensor_tensor(out=idxs[:, :], in0=bank[6][:, 0:32], scalar=-1.0,
                                            in1=rt[:, 0, 0:32], op0=ALU.add, op1=ALU.add))
                dve.sem_inc(route_done, 1)

            def experts(l, hid, hc):
                nhc = hid // hc
                per = [sum(1 for i in range(NT) if i % RING == s) for s in range(RING)]

                def evac_x(i, p):
                    dve.wait_ge(tx_mm, l * NT + i + 1)
                    if not (isinstance(i, int) and i < 2):
                        dve.wait_ge(g1_mm, l * NT + i - 1)
                    dst = xTs[0:KC, p, :, :]
                    src = bank[p][0:KC, 0:2 * P].rearrange("p (k t) -> p k t", k=NK)
                    if l == 0:
                        V.tensor_copy(dst, src).then_inc(tx_ev, 1)
                    else:
                        V.tensor_scalar(dst[:, 0, :], src[:, 0, :], gb[:, 0, 0:1], gb[:, 1, 0:1], ALU.mult, ALU.add)
                        V.tensor_scalar(dst[:, 1, :], src[:, 1, :], gb[:, 0, 1:2], gb[:, 1, 1:2],
                                        ALU.mult, ALU.add).then_inc(tx_ev, 1)

                def evac_h(i):
                    dve.wait_ge(th_mm, l * NT + i + 1)
                    if not (isinstance(i, int) and i == 0 and l == 0):
                        dve.wait_ge(g2_mm, l * NT + i)
                    if nhc * P <= 512:
                        V.tensor_copy(hTs[0:hc, 0:nhc * P], bank[4][0:hc, 0:nhc * P]).then_inc(th_ev, 1)
                    else:
                        V.tensor_copy(hTs[:, 0:384], bank[4][:, 0:384])
                        V.tensor_copy(hTs[:, 384:768], bank[5][:, 0:384]).then_inc(th_ev, 1)

                def evac_y(iv, s, first=False):
                    i = iv * RING + s
                    dve.wait_ge(g2_mm, l * NT + i + 1)
                    if not first:
                        dve.wait_ge(scat[s], 16 * (per[s] * l + iv))
                    V.tensor_scalar(ys[:, s, :], bank[6][:, 0:D], gs[:, bass.ds(i, 1)], None,
                                    ALU.mult).then_inc(y_ev, 1)

                evac_x(0, 0)
                evac_x(1, 1)

                def step(iv, s, first=False, xx=True):
                    if xx:
                        evac_x(iv * RING + s + 2, s % 2)
                    evac_h(iv * RING + s)
                    evac_y(iv, s, first=first)

                for s in range(RING):
                    step(0, s, first=(l == 0))
                last = NT // RING - 1
                with dve.Fori(1, last) as iv:
                    for s in range(RING):
                        step(iv, s)
                for s in range(RING):
                    step(last, s, xx=last * RING + s + 2 < NT)
                for s in range(NT - (last + 1) * RING):
                    step(last + 1, s, xx=(last + 1) * RING + s + 2 < NT)

            def add_acc(l):
                for p, buf in enumerate((xn, a1)):
                    dve.wait_ge(acc_ld[p], 16 * 9 * (l + 1))
                    link(V.tensor_tensor(h[:, :, :], h[:, :, :], buf[:, :, :], ALU.add))

            ln(2, h)
            xt_evac(2)
            route(0)
            V.memset(hTs[KC:KC + 1, 0:3 * P], 1.0)
            experts(0, HID0, HC0)
            add_acc(0)

            ln(3, h)
            xt_evac(3)
            V.memset(vb[:, :, :, KC:KC + 1], 1.0)
            link(V.memset(attT[KC:KC + 1, 1, :, :], 1.0))
            for j in range(NJ):
                dve.wait_ge(kv_mm, j + 1)
                V.tensor_scalar(kb[:, j, :], bank[2 + j % 4][:, 0:D], 0.0, float(HD) ** -0.5, ALU.max, ALU.add)
                V.tensor_copy(vb[:, j, :, 0:KC], bank[2 + j % 4][:, D:2 * D].rearrange("p (g n) -> p g n", g=NK)
                              ).then_inc(kv_ev, 1)
            for u in range(6):
                g, m = u // 2, u % 2
                dve.wait_ge(q_mm, u + 1)
                V.tensor_scalar(qT[:, m, 512 * g:512 * g + 512], bank[u % 2 + 6][0:KC, :], 0.0,
                                float(HD) ** -0.5, ALU.max, ALU.add).then_inc(q_ev, 1)
            mask = con[0:KC, C_MASK:C_MASK + KC]

            def state(b):
                dve.wait_ge(st_mm, b + 1)
                ps = bank[b % 2][0:KC, 0:2 * (KC + 1)].rearrange("p (g n) -> p g n", g=NK)
                if b >= 2:
                    dve.wait_ge(nd_mm, b - 1)
                V.tensor_tensor(kvm[:, b % 2], ps[:, :, 0:KC], mask.unsqueeze(1).to_broadcast([KC, NK, KC]), ALU.mult)
                V.tensor_scalar(ksm[:, b % 2, 0], mask, ps[:, 0, KC:KC + 1], None, ALU.mult)
                V.tensor_scalar(ksm[:, b % 2, 1], mask, ps[:, 1, KC:KC + 1], None, ALU.mult).then_inc(st_ev, 1)

            def ratio(b):
                dve.wait_ge(nd_mm, b + 1)
                num = bank[2 + 2 * (b % 2)][0:KC, 0:NK * T].rearrange("p (g t) -> p g t", g=NK)
                den = bank[3 + 2 * (b % 2)][0:KC, 0:NK * T].rearrange("p (g t) -> p g t", g=NK)
                link(V.tensor_scalar(rec, den, 1e-6, None, ALU.add))
                link(V.reciprocal(rec, rec))
                ins = V.tensor_tensor(attT[0:KC, :, b, :], num, rec, ALU.mult)
                ins.then_inc(att_ready, 1)
                dve.wait_ge(att_ready, b + 1)

            state(0)
            for b in range(B):
                if b + 1 < B:
                    state(b + 1)
                ratio(b)
            for j in range(NJ):
                dve.wait_ge(pr_mm, j + 1)
                last = V.tensor_tensor(h[:, j, :], h[:, j, :], bank[6 + j % 2][:, 0:D], ALU.add)
                last.then_inc(h_ready, 1)
            dve.wait_ge(h_ready, 2 + NJ)

            ln(4, h)
            for g in range(3):
                dve.wait_ge(xn_ready, 3 * NJ + 4 * g + 4)
                js = slice(4 * g, 4 * g + 4)
                V.tensor_tensor(h[:, js, :], h[:, js, :], xn[:, js, :], ALU.add)
                ln_start(xn, g)
            for g in range(3):
                ln_end(5, g)
            xt_evac(5)
            route(1)
            experts(1, HID1, HC1)
            add_acc(1)
            dve.sem_inc(fin_ready, 1)

        @block.tensor
        def _(pe):
            MM = nc.tensor.matmul

            def rows(k, biased=True):
                return KC + 1 if (k == NK - 1 and biased) else KC

            pe.wait_ge(ld_con, 16)
            pe.wait_ge(ld_patch, 32)
            for q in range(2):
                for jj in range(2):
                    j = 2 * q + jj
                    for k in range(4):
                        ins = MM(bank[q][:, jj * D:(jj + 1) * D], patchT[:, k, j * P:(j + 1) * P], projT[:, k, :],
                                 start=(k == 0), stop=(k == 3))
                ins.then_inc(patch_mm, 1)
            pe.wait_ge(ohl_ready, 1)
            pe.wait_ge(ld_seg, 16)
            for q in range(4):
                for jj in range(2):
                    b = 2 * q + jj
                    ins = MM(bank[2 + q][:, jj * D:(jj + 1) * D], ohl[:, b * NTXT:(b + 1) * NTXT], segt[:, :],
                             start=True, stop=True)
                ins.then_inc(seg_mm, 1)

            def transposes(n):
                m = XT_PASS[n]
                for q in range(NPAIR):
                    pe.wait_ge(xn_ready, (n - 1) * NJ + 2 * q + 2)
                    if m * NPAIR + q >= 2:
                        pe.wait_ge(xT_ready, m * NPAIR + q - 1)
                    for k in range(NK):
                        for jj in range(2):
                            ins = nc.tensor.transpose(bank[q % 2][0:KC, (2 * k + jj) * P:(2 * k + jj + 1) * P],
                                                      xn[:, 2 * q + jj, k * KC:(k + 1) * KC], ident)
                    ins.then_inc(xt_psum, 1)

            def logits(l):
                rw, biased = (rw0, True) if l == 0 else (rw1, False)
                pe.wait_ge(ld_rt, 16 * 6)
                for j in range(NJ):
                    pe.wait_ge(xT_ready, (1 if l == 0 else 3) * NPAIR + j // 2 + 1)
                    for k in range(NK):
                        r = rows(k, biased)
                        ins = MM(bank[7][:, j * NE:(j + 1) * NE], xT[0:r, k, j * P:(j + 1) * P], rw[0:r, k, :],
                                 start=(k == 0), stop=(k == NK - 1))
                ins.then_inc(lg_mm, 1)

            def ranks(l):
                pe.wait_ge(msk_ready, l + 1)
                m = msk[:, :, :].rearrange("p j e -> p (j e)")
                MM(bank[7][:, 96:192], con[:, C_TRI:C_TRI + P], m, start=True, stop=True)
                MM(bank[7][:, 192:288], con[:, C_ONE:C_ONE + P], m, start=True, stop=True).then_inc(rank_mm, 1)
                for a in range(NA):
                    if a % (NA // 4) == 0:
                        pe.wait_ge(one_ready, 4 * l + a // (NA // 4) + 1)
                    ins = MM(bank[6][:, 0:64], oneA[:, a, :], oneB[:, a, :, :].rearrange("p v q -> p (v q)"),
                             start=(a == 0), stop=(a == NA - 1))
                ins.then_inc(inv_mm, 1)

            def experts(l, hid, hc, w1, w2, biased):
                nhc = hid // hc
                nhalf = 1 if hid <= 512 else 2
                half = hid // nhalf
                w1v = w1.rearrange("p e k f -> p (e k f)")
                w2v = w2.rearrange("p e c n -> p (e c n)")

                def expert_of(i):
                    return pe.value_load(et[0:1, bass.ds(i, 1)], min_val=0, max_val=NE - 1)

                def t_x(iv, s):
                    per = sum(1 for i in range(NT) if i % RING == s)
                    i = iv * RING + s
                    pe.wait_ge(xs_ready[s], 16 * (l * per + iv + 1))
                    if not (isinstance(i, int) and i < 2 and l == 0):
                        pe.wait_ge(tx_ev, l * NT + i - 1)
                    for k in range(NK):
                        ins = nc.tensor.transpose(bank[s % 2][0:KC, k * P:(k + 1) * P],
                                                  xs[:, s, k * KC:(k + 1) * KC], ident)
                    ins.then_inc(tx_mm, 1)

                def g1(i, p, e):
                    pe.wait_ge(tx_ev, l * NT + i + 1)
                    if not (isinstance(i, int) and i == 0 and l == 0):
                        pe.wait_ge(act_done, l * NT + i)
                    for f in range(nhalf):
                        for k in range(NK):
                            r = rows(k, biased)
                            ins = MM(bank[2 + f][:, 0:half], xTs[0:r, p, k, :],
                                     w1v[0:r, bass.ds(e * (NK * hid) + (k * hid + f * half), half)],
                                     start=(k == 0), stop=(k == NK - 1))
                    ins.then_inc(g1_mm, 1)

                def t_h(i):
                    pe.wait_ge(act_done, l * NT + i + 1)
                    if not (isinstance(i, int) and i == 0 and l == 0):
                        pe.wait_ge(th_ev, l * NT + i)
                    for c in range(nhc):
                        bk, col = (bank[4], c * P) if nhc <= 4 else (bank[4 + c // 3], (c % 3) * P)
                        ins = nc.tensor.transpose(bk[0:hc, col:col + P], hact[:, c * hc:(c + 1) * hc], ident)
                    ins.then_inc(th_mm, 1)

                def g2(i, e):
                    pe.wait_ge(th_ev, l * NT + i + 1)
                    if not (isinstance(i, int) and i == 0 and l == 0):
                        pe.wait_ge(y_ev, l * NT + i)
                    for c in range(nhc):
                        r = hc + 1 if (c == nhc - 1 and biased) else hc
                        ins = MM(bank[6][:, 0:D], hTs[0:r, c * P:(c + 1) * P],
                                 w2v[0:r, bass.ds(e * (nhc * D) + c * D, D)],
                                 start=(c == 0), stop=(c == nhc - 1))
                    ins.then_inc(g2_mm, 1)

                pe.wait_ge(route_done, l + 1)
                pe.wait_ge(ones_ready, 1)
                pe.wait_ge(ld_ffn0 if l == 0 else ld_ffn1, 16 * (2 * NE + 2) if l == 0 else 16 * 2 * NE)
                t_x(0, 0)
                t_x(0, 1)
                g1(0, 0, expert_of(0))

                def step(iv, s, e, n_left):
                    i = iv * RING + s
                    if n_left > 2:
                        t_x(iv + (s + 2) // RING, (s + 2) % RING)
                    t_h(i)
                    nxt = None
                    if n_left > 1:
                        nxt = expert_of(i + 1)
                        g1(i + 1, (s + 1) % 2, nxt)
                    g2(i, e)
                    return nxt

                e = expert_of(0)
                for s in range(RING):
                    e = step(0, s, e, NT)
                last = NT // RING - 1
                with pe.Fori(1, last) as iv:
                    e = expert_of(iv * RING)
                    for s in range(RING):
                        e = step(iv, s, e, NT)
                e = expert_of(last * RING)
                for i in range(last * RING, NT):
                    e = step(i // RING, i % RING, e, NT - i)

            transposes(1)
            pe.wait_ge(ld_wst, 48)
            pe.wait_ge(ones_ready, 1)
            for g in range(3):
                pe.wait_ge(xT_ready, 2 * (g + 1))
                for cc in range(4):
                    u = 4 * g + cc
                    if u < 4:
                        pass
                    if u >= 6:
                        v = u - 6
                        pe.wait_ge(ev_act, v + 1)
                        if v % 4:
                            pe.wait_ge(ev_dve, 3 * (v // 4) + v % 4)
                    for k in range(NK):
                        r = rows(k)
                        ins = MM(bank[2 + u % 6][:, :], wst[0:r, k, cc, :], xT[0:r, k, 512 * g:512 * g + 512],
                                 start=(k == 0), stop=(k == NK - 1))
                    ins.then_inc(proj_mm, 1)
            pe.wait_ge(scanned, 1)
            for q in range(2):
                for c in range(3):
                    for a in range(2):
                        ins = MM(bank[q][NPATCH * a:NPATCH * (a + 1), c * P:(c + 1) * P],
                                 hist[:, 1:NPATCH + 1, 2 * q + a, c], ident, start=True, stop=True)
                ins.then_inc(back_mm, 1)
            for ch in range(NCH):
                for c in range(3):
                    ins = nc.tensor.transpose(bank[2 + ch][:, c * P:(c + 1) * P], hist[:, NPATCH + 1:T + 1, ch, c],
                                              ident)
                ins.then_inc(back_mm, 1)

            transposes(2)
            logits(0)
            ranks(0)
            experts(0, HID0, HC0, w1a, w2a, True)

            transposes(3)
            pe.wait_ge(ld_attn, 16 * 5)
            for j in range(NJ):
                pe.wait_ge(xT_ready, 2 * NPAIR + j // 2 + 1)
                if j >= 4:
                    pe.wait_ge(kv_ev, j - 3)
                for k in range(NK):
                    ins = MM(bank[2 + j % 4][:, 0:2 * D], xT[0:KC, k, j * P:(j + 1) * P], qkvw[:, k, D:3 * D],
                             start=(k == 0), stop=(k == NK - 1))
                ins.then_inc(kv_mm, 1)
            for u in range(6):
                g, m = u // 2, u % 2
                if u >= 2:
                    pe.wait_ge(q_ev, u - 1)
                for k in range(NK):
                    ins = MM(bank[u % 2 + 6][0:KC, :], qkvw[:, k, m * KC:(m + 1) * KC],
                             xT[0:KC, k, 512 * g:512 * g + 512], start=(k == 0), stop=(k == NK - 1))
                ins.then_inc(q_mm, 1)

            def sums(b):
                if b >= 2:
                    pe.wait_ge(st_ev, b - 1)
                ph = slice(NPATCH * (b % 2), NPATCH * (b % 2) + NPATCH)
                for g in range(NK):
                    o_ = bank[b % 2][0:KC, g * (KC + 1):(g + 1) * (KC + 1)]
                    MM(o_, kb[:, NPJ + b, g * KC:(g + 1) * KC], vb[:, NPJ + b, g, :], start=True, stop=False)
                    ins = MM(o_, kb[ph, b // 2, g * KC:(g + 1) * KC], vb[ph, b // 2, g, :], start=False, stop=True)
                ins.then_inc(st_mm, 1)

            def numden(b):
                pe.wait_ge(st_ev, b + 1)
                if b >= 2:
                    pe.wait_ge(att_ready, b - 1)
                for w, m in enumerate((kvm, ksm)):
                    o_ = bank[2 + 2 * (b % 2) + w]
                    for g in range(NK):
                        MM(o_[0:KC, g * T:g * T + NPATCH], m[:, b % 2, g, :], qT[:, g, NPATCH * b:NPATCH * (b + 1)],
                           start=True, stop=True)
                        ins = MM(o_[0:KC, g * T + NPATCH:(g + 1) * T], m[:, b % 2, g, :],
                                 qT[:, g, 512 + NTXT * b:512 + NTXT * (b + 1)], start=True, stop=True)
                ins.then_inc(nd_mm, 1)

            pe.wait_ge(kv_ev, NJ)
            pe.wait_ge(q_ev, 6)
            sums(0)
            for b in range(B):
                if b + 1 < B:
                    sums(b + 1)
                numden(b)
            for j in range(NJ):
                if j == 0:
                    pe.wait_ge(att_ready, B)
                if j >= 2:
                    pe.wait_ge(h_ready, 2 + j - 1)
                if j < NPJ:
                    parts = [(slice(NPATCH * a, NPATCH * (a + 1)), attT[:, :, 2 * j + a, 0:NPATCH])
                             for a in range(2)]
                else:
                    parts = [(slice(0, P), attT[:, :, j - NPJ, NPATCH:T])]
                for pr, a in parts:
                    for g in range(NK):
                        ins = MM(bank[6 + j % 2][pr, 0:D], a[0:rows(g), g], prw[0:rows(g), g, :],
                                 start=(g == 0), stop=(g == NK - 1))
                ins.then_inc(pr_mm, 1)

            transposes(5)
            logits(1)
            ranks(1)
            experts(1, HID1, HC1, w1b, w2b, False)


def constants():
    c = np.zeros((P, NCONST), np.float32)
    p = np.arange(P)
    c[:, C_ID:C_ID + P] = np.eye(P)
    c[:, C_TRI:C_TRI + P] = p[:, None] < p[None, :]
    c[:, C_ONE:C_ONE + P] = 1.0
    e = np.arange(KC)
    c[:KC, C_MASK:C_MASK + KC] = e[:, None] // HD == e[None, :] // HD
    c[:, C_IOTA:C_IOTA + P] = p[None, :]
    c[:, C_THR:C_THR + NJ] = P * np.arange(NJ)[None, :]
    c[:, C_RST:C_RST + NE * NJ] = (np.arange(NE * NJ) % NJ != 0)[None, :]
    for j in range(NJ):
        if j < NPJ:
            row = (2 * j + p // NPATCH) * T + p % NPATCH
        else:
            row = (j - NPJ) * T + NPATCH + p
        c[:, C_TOK + j] = row + 1
    c[:, C_PAD] = NTOK + 1 + p
    c[:, C_EPS] = EPS
    c[:, C_HPI] = np.pi / 2
    c[:, C_PART] = p
    pos = np.arange(NTXT, dtype=np.float32)[:, None]
    i = np.arange(D, dtype=np.float32)[None, :]
    angle = pos / np.power(np.float32(10000.0), (np.floor(i / np.float32(2.0)) * np.float32(2.0) / np.float32(D)))
    sinpos = np.where(np.arange(D) % 2 == 0, np.sin(angle), np.cos(angle)).astype(np.float32)
    return c, sinpos


def kernel(**inp):
    import concourse.bacc as bacc
    from concourse.bass_utils import run_bass_kernel_spmd

    a = {k: np.asarray(v) for k, v in inp.items()}
    con, sinpos = constants()
    arr = {"consts": con, "sinpos": sinpos}
    n = 128 // 16
    patches = a["x"].reshape(B, 2, n, 16, n, 16).transpose(0, 1, 2, 4, 3, 5).reshape(B * NPATCH, PD).T
    arr["patchT"] = patches
    arr["projT"] = a["L0_tok_proj_w"].T
    arr["projb"] = a["L0_tok_proj_b"].reshape(D)
    arr["pos"] = a["L0_tok_pos_emb"].reshape(NPATCH, D)
    arr["labels"] = a["mask_BS_i2_0"].reshape(B * NTXT)
    arr["ids"] = a["x_txt"].T
    arr["table"] = a["L0_txt_token_table"]
    arr["segm"] = a["L0_txt_segm_table"]
    wb = a["L0_attn_W_biv"].reshape(NB, 3, D).transpose(2, 1, 0)
    wi = a["L0_attn_W_in"].reshape(NB, 3, D).transpose(2, 1, 0)
    wd = np.repeat(a["L0_attn_W_decay"].T, P, axis=1).reshape(D, 1, P)
    arr["wst"] = np.concatenate([wd, np.concatenate([wb, wi], axis=2)], axis=1)
    bb = a["L0_attn_b_biv"].reshape(NB, 3).T
    bi = a["L0_attn_b_in"].reshape(NB, 3).T
    bd = np.repeat(a["L0_attn_b_decay"], P).reshape(1, P)
    arr["wst_b"] = np.concatenate([bd, np.concatenate([bb, bi], axis=1)], axis=0)[None]
    arr["rw0"], arr["rb0"] = a["L0_ffn_router_w"], a["L0_ffn_router_b"].reshape(1, NE)
    arr["w1a"], arr["b1a"] = a["L0_ffn_w1"], a["L0_ffn_b1"]
    arr["w2a"], arr["b2a"] = a["L0_ffn_w2"], a["L0_ffn_b2"]
    arr["qkvT"], arr["prT"] = a["L1_attn_qkv_w"].T, a["L1_attn_proj_w"].T
    arr["prb"] = a["L1_attn_proj_b"].reshape(1, D)
    g = a["L1_ffn_ln_gamma"].reshape(NK, KC).T
    be = a["L1_ffn_ln_beta"].reshape(NK, KC).T
    arr["gb"] = np.stack([g, be], axis=1)
    arr["rw1"] = a["L1_ffn_router_w"]
    arr["w1b"], arr["w2b"] = a["L1_ffn_w1"], a["L1_ffn_w2"]

    nc = bacc.Bacc("TRN2", target_bir_lowering=False, num_devices=1)
    arrays, aps = {}, {}
    for k, v in arr.items():
        v = np.ascontiguousarray(v)
        arrays["in_" + k] = v
        aps[k] = nc.dram_tensor("in_" + k, v.shape, mybir.dt.from_np(v.dtype), kind="ExternalInput").ap()
    out = nc.dram_tensor("out", (NTOK, D), F32, kind="ExternalOutput").ap()
    build(nc, aps, out)
    r = run_bass_kernel_spmd(nc, [arrays], core_ids=[0])
    return r.results[0]["out"].reshape(B, T, D)
```

```python
from contextlib import ExitStack

import numpy as np

import concourse.bass as bass
from concourse import mybir

F32 = mybir.dt.float32
BF16 = mybir.dt.bfloat16
I32 = mybir.dt.int32
U32 = mybir.dt.uint32
ALU = mybir.AluOpType
ACT = mybir.ActivationFunctionType
AX = mybir.AxisListType.X

P = 128
B, NPATCH, NTXT, D = 8, 64, 128, 192
T = NPATCH + NTXT
NTOK = B * T
NJ = NTOK // P
NPJ = B * NPATCH // P
KC = 96
NK = D // KC
PD = 512
VOCAB, NSEG = 8000, 3
NB = D // 3
NCH = 4
NE = 8
TOPK = 2
NA = TOPK * NJ
NT = NTOK * TOPK // P + NE - 1
HID0, HID1 = 288, 768
HC0, HC1 = 96, 128
NH, HD = 12, 16
ROWS = NTOK + P
EPS = 1e-5
TCH = 64
NCHUNK = T // TCH
RING = 4
NV = 5

TWO_PI = 2.0 * np.pi
C1 = 6.28125
C2 = TWO_PI - C1
MAGIC = 1.5 * 2.0 ** 23
PI_DOWN = 3.1415925

C_ID, C_TRI, C_ONE, C_IOTA, C_MASK = 0, P, 2 * P, 3 * P, 4 * P
KV = KC + KC // HD
C_THR = C_MASK + KV
C_RST = C_THR + NJ
C_TOK = C_RST + NE * NJ
C_PAD = C_TOK + 2 * NJ
C_EPS, C_HPI, C_PART = C_PAD + 1, C_PAD + 2, C_PAD + 3
NCONST = C_PART + 1


def build(nc, x, out):
    ctx = ExitStack()
    with ctx:
        def sb(name, shape, dt=F32):
            return ctx.enter_context(nc.sbuf_tensor(name, shape, dt))

        def sem(name):
            return ctx.enter_context(nc.semaphore(name))

        class Chain:

            def __init__(self, eng, s):
                self.eng, self.sem, self.n = eng, s, 0

            def __call__(self, ins):
                self.n += 1
                ins.then_inc(self.sem, 1)
                self.eng.wait_ge(self.sem, self.n)

        xd = nc.dram_tensor("xn_rows", [ROWS, D], F32, kind="Internal").ap()
        acc = [nc.dram_tensor(f"acc{p}", [ROWS, D], F32, kind="Internal").ap() for p in range(2)]
        sums_of = [acc, [out, out]]
        DIST = [2, 1]

        con = sb("con", [P, NCONST])
        ident = con[:, C_ID:C_ID + P]
        iota = con[:, C_IOTA:C_IOTA + P]
        sinpos = sb("sinpos", [P, D])
        bp = sb("bp", [P, 2, D])
        h = sb("h", [P, NJ, D])
        xn = sb("xn", [P, NJ, D])
        a1 = sb("a1", [P, NJ, D])
        xT = sb("xT", [KC + 1, NK, NTOK])
        st = sb("st", [P, NJ, 6])
        mv = sb("mv", [P, NJ, 2])
        std = sb("std", [P, NJ])
        rstd = sb("rstd", [P, NJ])
        nmr = sb("nmr", [P, NJ])
        ids = sb("ids", [P, B], I32)
        ids2 = sb("ids2", [P, B], I32)
        segt = sb("segt", [NSEG, D])
        wst = sb("wst", [KC + 1, NK, 4, P])
        rw0 = sb("rw0", [KC + 1, NK, NE])
        rw1 = sb("rw1", [KC + 1, NK, NE])
        rwg = sb("rwg", [KC + 1, NK, NE])
        z = sb("z", [P, 3, NH])
        gb = sb("gb", [KC, 2, NK])
        qkvw = sb("qkvw", [KC, NK, 3 * D])
        prw = sb("prw", [KC + 1, NK, D])
        lgs = sb("lgs", [P, NJ, NE])
        mx = sb("mx", [P, NJ, 8])
        ix = sb("ix", [P, NJ, 8], U32)
        ex = sb("ex", [P, NJ, NE + 2])
        idxf = sb("idxf", [P, NJ, 2])
        oh = sb("oh", [P, 2, NJ, NE])
        msk = sb("msk", [P, NJ, NE])
        gate = sb("gate", [P, 2, NJ])
        sm = sb("sm", [P, 3, NJ])
        rt = sb("rt", [P, 4, NE * NJ])
        te = sb("te", [P, 4, NE])
        slf = sb("slf", [P, 4, NA])
        sli = sb("sli", [P, 3, NA], I32)
        iotab = sb("iotab", [P, P], BF16)
        valb = sb("valb", [P, NV, 2, NJ], BF16)
        tileb = sb("tileb", [P, NA], BF16)
        gres = sb("gres", [P, 2, 2, NJ])
        idxs = sb("idxs", [P, 32], I32)
        gs = sb("gs", [P, 32])
        etf = sb("etf", [1, 2, 32])
        et = sb("et", [1, 32], I32)
        gidx = sb("gidx", [P, RING], I32)
        sidx = sb("sidx", [P, RING], I32)
        xTs = sb("xTs", [KC + 1, 2, NK, P])

        NR1 = 23360
        reg1 = sb("reg1", [P, NR1])
        o = 0

        def carve(reg, n):
            nonlocal o
            o += n
            return reg[:, o - n:o]

        Mt = carve(reg1, T * NCH * 12).rearrange("p (t a r c) -> p t a r c", a=NCH, r=3, c=4)
        hist = carve(reg1, (T + 1) * NCH * 4).rearrange("p (t a c) -> p t a c", a=NCH, c=4)
        biv = carve(reg1, 3 * NCH * T).rearrange("p (c a t) -> p c a t", c=3, a=NCH)
        dec = carve(reg1, NCH * T).rearrange("p (a t) -> p a t", a=NCH)
        U = NCH * TCH

        def unit(n):
            v = carve(reg1, n * U)
            return v.rearrange("p (c a t) -> p c a t", c=n, a=NCH)

        sq, th, rk, yy, nn = unit(3), unit(2), unit(1), unit(1), unit(2)
        trig, kc4, dd = unit(3), unit(4), unit(3)
        sk, wk, dg, off = unit(3), unit(3), unit(3), unit(3)
        prod = carve(reg1, NCH * 12)
        assert o <= NR1
        o = 0
        w1b = carve(reg1, NE * NK * HID1)[0:KC, :].rearrange("p (e k f) -> p e k f", e=NE, k=NK)
        w2b = carve(reg1, NE * (HID1 // HC1) * D).rearrange("p (e c n) -> p e c n", e=NE, n=D)
        o = 0
        patchT = carve(reg1, 4 * PD).rearrange("p (k t) -> p k t", k=4)
        projT = carve(reg1, 4 * D).rearrange("p (k n) -> p k n", k=4)
        lab = carve(reg1, B * NTXT)[0:NSEG, :].bitcast(I32)
        lab2 = carve(reg1, B * NTXT)[0:NSEG, :].bitcast(I32)
        lab3 = carve(reg1, B * NTXT)[0:NSEG, :].bitcast(I32)
        ohl = carve(reg1, B * NTXT)[0:NSEG, :]
        zero = a1[:, 0, :]
        w1r = xT[0:KC, :, :].rearrange("p k t -> p (k t)").rearrange("p (b k f) -> p b k f", b=2, k=NK)

        NR2 = NE * NK * HID0 + NE * (HID0 // HC0) * D
        reg2 = sb("reg2", [P, NR2])
        o = 0
        w1a = carve(reg2, NE * NK * HID0)[0:KC + 1, :].rearrange("p (e k f) -> p e k f", e=NE, k=NK)
        w2a = carve(reg2, NE * (HID0 // HC0) * D)[0:KC + 1, :].rearrange("p (e c n) -> p e c n", e=NE, n=D)
        o = 0
        qT = carve(reg2, NK * NTOK)[0:KC, :].rearrange("p (g t) -> p g t", g=NK)
        kb = carve(reg2, NJ * D).rearrange("p (j n) -> p j n", j=NJ)
        vb = carve(reg2, NJ * NK * KV).rearrange("p (j n) -> p j n", n=KV)
        kvm = carve(reg2, 2 * 4 * KV)[0:KC, :].rearrange("p (i a n) -> p i a n", i=2, a=4)
        assert o <= NR2

        reg3 = sb("reg3", [P, NA * P])
        oneA = reg3[:, 0:NA * P // 2].bitcast(BF16).rearrange("p (a r) -> p a r", a=NA)
        oneT = reg3[:, NA * P // 2:NA * (P + 32) // 2].bitcast(BF16).rearrange("p (a q) -> p a q", a=NA)
        oneB = a1[:, :, :].rearrange("p j n -> p (j n)")[:, 0:NA * NV * 16].bitcast(BF16).rearrange(
            "p (a v q) -> p a v q", a=NA, v=NV)
        attT = reg3[0:KC + 1, 0:NK * NTOK].rearrange("p (g t) -> p g t", g=NK)
        att = a1
        o = 0
        hact = carve(reg3, HID1)
        hTs = carve(reg3, HID1)
        hT2 = reg3[:, 0:2 * HID1].rearrange("p (b f) -> p b f", b=2)
        xs = carve(reg3, RING * D).rearrange("p (s n) -> p s n", s=RING)
        ys = carve(reg3, RING * D).rearrange("p (s n) -> p s n", s=RING)

        bank = [ctx.enter_context(nc.psum_tensor(f"bank{i}", [P, 512], F32)) for i in range(8)]

        ld_con = sem("ld_con"); ld_lab = sem("ld_lab"); ld_ids = sem("ld_ids"); ld_seg = sem("ld_seg")
        ld_patch = sem("ld_patch"); ld_pos = sem("ld_pos"); ld_wst = sem("ld_wst")
        ld_ffn0 = sem("ld_ffn0"); ld_attn = sem("ld_attn"); ld_ffn1 = sem("ld_ffn1"); ld_rt = sem("ld_rt")
        zero_ready = sem("zero_ready"); zero_done = sem("zero_done"); bzero_done = sem("bzero_done")
        ids_ready = sem("ids_ready"); ohl_ready = sem("ohl_ready")
        gath = [sem(f"gath{q}") for q in range(4)]
        patch_mm = sem("patch_mm"); seg_mm = sem("seg_mm")
        ones_ready = sem("ones_ready")
        dve_self = sem("dve_self"); act_self = sem("act_self"); pool_self = sem("pool_self"); pool_turn = sem("pool_turn")
        scan_self = sem("scan_self")
        var_ready = [sem("var_ready"), sem("var5_ready")]
        std_ready = [sem("std_ready"), sem("std5_ready")]
        rstd_ready = [sem("rstd_ready"), sem("rstd5_ready")]
        xn_ready = sem("xn_ready"); xn5_ready = sem("xn5_ready")
        xt_psum = sem("xt_psum"); xT_ready = sem("xT_ready")
        h_ready = sem("h_ready")
        proj_mm = sem("proj_mm"); ev_act = sem("ev_act"); ev_dve = sem("ev_dve")
        sq_ready = sem("sq_ready"); th2_ready = sem("th2_ready"); th_ready = sem("th_ready")
        rk_ready = sem("rk_ready"); y_ready = sem("y_ready"); trig_ready = sem("trig_ready")
        m_ready = sem("m_ready")
        scanned = sem("scanned"); back_mm = sem("back_mm")
        xd_written = sem("xd_written")
        lg_mm = sem("lg_mm"); ex_in = sem("ex_in"); ex_out = sem("ex_out"); msk_ready = sem("msk_ready")
        rank_mm = sem("rank_mm"); one_ready = sem("one_ready"); oneB_ready = sem("oneB_ready"); gate_ready = sem("gate_ready")
        slot_ready = sem("slot_ready"); oneP_ready = sem("oneP_ready"); gpart_ready = sem("gpart_ready"); inv_mm = sem("inv_mm")
        route_done = sem("route_done")
        gidx_ready = sem("gidx_ready"); sidx_ready = sem("sidx_ready")
        xs_ready = [sem(f"xs_ready{s}") for s in range(RING)]
        scat = [sem(f"scat{s}") for s in range(RING)]
        tx_mm = sem("tx_mm"); tx_ev = sem("tx_ev"); g1_mm = sem("g1_mm"); act_done = sem("act_done")
        w1r_act = sem("w1r_act"); w1r_dve = sem("w1r_dve")
        th_mm = sem("th_mm"); th_ev = sem("th_ev"); g2_mm = sem("g2_mm"); y_ev = sem("y_ev")
        acc_ld = [sem(f"acc_ld{g}") for g in range(2)]
        kv_mm = sem("kv_mm"); k_ev = sem("k_ev"); v_ev = sem("v_ev"); q_mm = sem("q_mm"); q_ev = sem("q_ev")
        bb_ready = sem("bb_ready"); bias_mm = sem("bias_mm"); rwg_ready = sem("rwg_ready")
        st_mm = sem("st_mm"); st_ev = sem("st_ev"); nd_mm = sem("nd_mm"); att_ready = sem("att_ready")
        at_mm = sem("at_mm"); at_ev = sem("at_ev")
        res_done = sem("res_done"); xt5_mm = sem("xt5_mm"); xT5_ready = sem("xT5_ready")
        pr_mm = sem("pr_mm"); stored = sem("stored")

        block = ctx.enter_context(nc.Block())

        NPAIR = NJ // 2
        NBP = B // 2
        LG_BANK = [6, 7, 5, 4]
        NAP = 8
        XT_PASS = {1: 0, 2: 1, 3: 2}

        def trio(i):
            return [i, NPJ + 2 * i, NPJ + 2 * i + 1]

        GROUPS = {n: [list(range(4 * g, 4 * g + 4)) for g in range(3)] for n in (1, 2, 3)}
        GROUPS[4] = GROUPS[5] = [trio(i) for i in range(NBP)]

        def ln_sem(n, g):
            return (0, 3 * (n - 1) + g + 1) if n < 5 else (1, g + 1)

        def ln_cols(n, g):
            m = len(GROUPS[n][0])
            return slice(m * g, m * g + m)

        def tok_rows(dram, buf):
            dv = dram[0:NTOK, :].rearrange("(b t) n -> b t n", b=B)
            pairs = [(dv[a::2, 0:NPATCH, :].rearrange("b t n -> t b n"), buf[NPATCH * a:NPATCH * (a + 1), 0:NPJ, :])
                     for a in range(2)]
            pairs.append((dv[:, NPATCH:T, :].rearrange("b t n -> t b n"), buf[:, NPJ:NJ, :]))
            return pairs

        def prep_angle(eng, ns, link, c):
            tt, ts = ns.tensor_tensor, ns.tensor_scalar
            eng.wait_ge(sq_ready, c + 1)
            link(tt(th[:, 0], sq[:, 0], sq[:, 1], ALU.add))
            tt(th[:, 0], th[:, 0], sq[:, 2], ALU.add).then_inc(th2_ready, 1)
            eng.wait_ge(th_ready, c + 1)
            link(ts(yy[:, 0], th[:, 1], float(1.0 / TWO_PI), MAGIC, ALU.mult, ALU.add))
            ts(nn[:, 0], yy[:, 0], MAGIC, -C1, ALU.subtract, ALU.mult)
            link(ts(nn[:, 1], yy[:, 0], MAGIC, -C2, ALU.subtract, ALU.mult))
            link(tt(nn[:, 0], nn[:, 0], th[:, 1], ALU.add))
            link(tt(yy[:, 0], nn[:, 0], nn[:, 1], ALU.add))
            ts(yy[:, 0], yy[:, 0], -PI_DOWN, PI_DOWN, ALU.max, ALU.min).then_inc(y_ready, 1)

        def prep_matrix(eng, ns, link, c):
            tt = ns.tensor_tensor
            t0 = c * TCH
            b3 = [P, 3, NCH, TCH]
            eng.wait_ge(rk_ready, c + 1)
            tt(kc4[:, 0:3], biv[:, :, :, t0:t0 + TCH], rk[:, 0:1].to_broadcast(b3), ALU.mult)
            link(tt(kc4[:, 3], biv[:, 0, :, t0:t0 + TCH], rk[:, 0], ALU.mult))
            eng.wait_ge(trig_ready, c + 1)
            d = dec[:, :, t0:t0 + TCH]
            tt(dd[:, 0], trig[:, 0], d, ALU.mult)
            link(tt(dd[:, 1], trig[:, 2], d, ALU.mult))
            link(tt(dd[:, 2], d, dd[:, 1], ALU.subtract))
            tt(sk, kc4[:, 0:3], dd[:, 0:1].to_broadcast(b3), ALU.mult)
            link(tt(wk, kc4[:, 0:3], dd[:, 2:3].to_broadcast(b3), ALU.mult))
            tt(dg, wk, kc4[:, 0:3], ALU.mult)
            link(tt(off, wk, kc4[:, 1:4], ALU.mult))

            def ent(r, cc):
                return Mt[:, t0:t0 + TCH, :, r, cc].rearrange("p t a -> p a t")

            for r in range(3):
                tt(ent(r, r), dg[:, r], dd[:, 1], ALU.add)
            last = None
            for r in range(3):
                q, s = (r + 1) % 3, (r + 2) % 3
                tt(ent(r, q), off[:, r], sk[:, s], ALU.subtract)
                last = tt(ent(q, r), off[:, r], sk[:, s], ALU.add)
            link(last)
            eng.sem_inc(m_ready, 1)

        def trig_of(act, link, c):
            t0 = c * TCH
            act.wait_ge(ev_dve, 3 if c == 0 else 9)
            nc.scalar.activation(sq, biv[:, :, :, t0:t0 + TCH], ACT.Square).then_inc(sq_ready, 1)
            act.wait_ge(th2_ready, c + 1)
            nc.scalar.activation(th[:, 1], th[:, 0], ACT.Sqrt).then_inc(th_ready, 1)
            act.wait_ge(y_ready, c + 1)
            nc.scalar.activation(trig[:, 0], yy[:, 0], ACT.Sin)
            link(nc.scalar.activation(trig[:, 1], yy[:, 0], ACT.Abs))
            nc.scalar.activation(trig[:, 2], trig[:, 1], ACT.Sin, bias=con[:, C_HPI:C_HPI + 1],
                                 scale=-1.0).then_inc(trig_ready, 1)

        def recip_of(dve, V, link, c):
            dve.wait_ge(th_ready, c + 1)
            link(V.tensor_scalar(rk[:, 0], th[:, 1], 1e-8, None, ALU.max))
            V.reciprocal(rk[:, 0], rk[:, 0]).then_inc(rk_ready, 1)

        @block.sync
        def _(sp):
            sp.dma_start(con[:, :], x["consts"]).then_inc(ld_con, 16)
            sp.dma_start(patchT, x["patchT"].rearrange("(k p) t -> p k t", p=P)).then_inc(ld_patch, 16)
            sp.dma_start(projT, x["projT"].rearrange("(k p) n -> p k n", p=P)).then_inc(ld_patch, 16)
            for k in range(NK):
                sp.dma_start(wst[0:KC, k, :, :], x["wst"][k * KC:(k + 1) * KC, :, :]).then_inc(ld_wst, 16)
            sp.dma_start(wst[KC:KC + 1, 1, :, :], x["wst_b"]).then_inc(ld_wst, 16)
            sp.wait_ge(xn_ready, NJ)
            sp.wait_ge(zero_ready, 1)
            for p in range(2):
                sp.dma_start(acc[p].rearrange("(a p) n -> p a n", p=P),
                             zero.unsqueeze(1).to_broadcast([P, ROWS // P, D])).then_inc(zero_done, 16)
            sp.dma_start(xd[NTOK:ROWS, :], zero).then_inc(zero_done, 16)
            sp.dma_start(out[NTOK:ROWS, :], zero).then_inc(zero_done, 16)
            for e in range(NE):
                sp.dma_start(w1a[0:KC, e, :, :], x["w1a"][e].rearrange("(k p) f -> p k f", p=KC)).then_inc(ld_ffn0, 16)
                sp.dma_start(w2a[0:KC, e, :, :], x["w2a"][e].rearrange("(c p) n -> p c n", p=KC)).then_inc(ld_ffn0, 16)
            sp.dma_start(w1a[KC:KC + 1, :, 1, :], x["b1a"].rearrange("(a e) f -> a e f", a=1)).then_inc(ld_ffn0, 16)
            sp.dma_start(w2a[KC:KC + 1, :, 2, :], x["b2a"].rearrange("(a e) n -> a e n", a=1)).then_inc(ld_ffn0, 16)

            def write_rows(n):
                for dst, src in tok_rows(xd, xn):
                    sp.dma_start(dst, src).then_inc(xd_written, 16)

            def wait_scatters(l):
                for s in range(RING):
                    sp.wait_ge(scat[s], 16 * (sum(1 for i in range(NT) if i % RING == s) * (l + 1)))

            sp.wait_ge(xn_ready, 2 * NJ)
            write_rows(0)
            wait_scatters(0)
            for p, buf in enumerate((xn, a1)):
                for dr, sbuf in tok_rows(acc[p], buf):
                    sp.dma_start(sbuf, dr).then_inc(acc_ld[p], 16)
            for e in range(NE):
                sp.dma_start(w1b[:, e, :, :], x["w1b"][e].rearrange("(k p) f -> p k f", p=KC)).then_inc(ld_ffn1, 16)
                sp.dma_start(w2b[:, e, :, :], x["w2b"][e].rearrange("(c p) n -> p c n", p=HC1)).then_inc(ld_ffn1, 16)
            sp.wait_ge(xn5_ready, NJ)
            write_rows(1)
            sp.wait_ge(res_done, NBP)
            for dr, sbuf in tok_rows(out, h):
                sp.dma_start(dr, sbuf).then_inc(stored, 16)
            sp.wait_ge(stored, 16 * 3)
            wait_scatters(1)

        @block.gpsimd
        def _(pool):
            link = Chain(pool, pool_self)
            nc.gpsimd.memset(zero, 0.0).then_inc(zero_ready, 1)
            pool.wait_ge(ids_ready, 1)
            for b in range(B):
                pool.indirect_dma_start(xn[:, NPJ + b, :], None, x["table"],
                                        bass.IndirectOffsetOnAxis(ap=ids2[:, b:b + 1], axis=0)
                                        ).then_inc(gath[b // 2], 16)

            for c in range(1, NCHUNK):
                prep_angle(pool, nc.gpsimd, link, c)
                prep_matrix(pool, nc.gpsimd, link, c)

            def route_share(l):
                G = nc.gpsimd
                pool.wait_ge(gate_ready, l + 1)
                link(G.tensor_copy(valb[:, 2], gate[:, :, :]))
                link(G.tensor_tensor(gres[:, 0], gate[:, :, :], valb[:, 2], ALU.subtract))
                link(G.tensor_copy(valb[:, 3], gres[:, 0]))
                link(G.tensor_tensor(gres[:, 1], gres[:, 0], valb[:, 3], ALU.subtract))
                G.tensor_copy(valb[:, 4], gres[:, 1]).then_inc(gpart_ready, 1)
                pool.wait_ge(slot_ready, l + 1)
                for a in range(NAP):
                    G.tensor_scalar(oneA[:, a, :], iotab[:, :], slf[:, 2, a:a + 1], None,
                                    ALU.is_equal).then_inc(oneP_ready, 1)

            def expert_dma(l):
                base = {s: l * sum(1 for i in range(NT) if i % RING == s) for s in range(RING)}

                def gather(iv, s):
                    pool.wait_ge(gidx_ready, l * NT + iv * RING + s + 1)
                    pool.sem_inc(pool_turn, 1)
                    pool.indirect_dma_start(xs[:, s, :], None, xd,
                                            bass.IndirectOffsetOnAxis(ap=gidx[:, s:s + 1], axis=0)
                                            ).then_inc(xs_ready[s], 16)

                def scatter(iv, s):
                    i = iv * RING + s
                    pool.wait_ge(sidx_ready, l * NT + i + 1)
                    pool.wait_ge(y_ev, l * NT + i + 1)
                    s2 = (s - DIST[l]) % RING
                    n = base[s2] + iv + (1 if s >= DIST[l] else 0)
                    if not (isinstance(n, int) and n == 0):
                        pool.wait_ge(scat[s2], 16 * n)
                    pool.sem_inc(pool_turn, 1)
                    pool.indirect_dma_start(sums_of[l][s % 2],
                                            bass.IndirectOffsetOnAxis(ap=sidx[:, s:s + 1], axis=0),
                                            ys[:, s, :], None, compute_op=ALU.add).then_inc(scat[s], 16)

                pool.wait_ge(xd_written, 16 * 3 * (l + 1))
                pool.wait_ge(zero_done, 16 * 4)
                if l:
                    pool.wait_ge(stored, 16 * 3)
                for s in range(RING):
                    gather(0, s)
                for s in range(RING):
                    gather(1, s)
                    scatter(0, s)
                with pool.Fori(1, NT // RING - 1) as iv:
                    for s in range(RING):
                        gather(iv + 1, s)
                        scatter(iv, s)
                last = NT // RING - 1
                for s in range(RING):
                    if (last + 1) * RING + s < NT:
                        gather(last + 1, s)
                    scatter(last, s)
                for s in range(NT - (last + 1) * RING):
                    scatter(last + 1, s)

            for l in range(2):
                route_share(l)
                expert_dma(l)

        @block.scalar
        def _(act):
            link = Chain(act, act_self)
            act.dma_start(lab, x["labels"].partition_broadcast(NSEG)).then_inc(ld_lab, 16)
            act.dma_start(ids[:, :], x["ids"]).then_inc(ld_ids, 16)
            act.dma_start(segt[:, :], x["segm"]).then_inc(ld_seg, 16)
            act.dma_start(sinpos[:, :], x["sinpos"]).then_inc(ld_pos, 16)
            act.dma_start(bp[0:NPATCH, 0, :], x["pos"]).then_inc(ld_pos, 16)
            act.dma_start(bp[NPATCH:P, 0, :], x["pos"]).then_inc(ld_pos, 16)
            act.dma_start(bp[:, 1, :], x["projb"].partition_broadcast(P)).then_inc(ld_pos, 16)
            for k in range(NK):
                rows = slice(k * KC, (k + 1) * KC)
                act.dma_start(rw0[0:KC, k, :], x["rw0"][rows, :]).then_inc(ld_rt, 16)
                act.dma_start(rw1[0:KC, k, :], x["rw1"][rows, :]).then_inc(ld_rt, 16)
                act.dma_start(qkvw[:, k, :], x["qkvT"][rows, :]).then_inc(ld_attn, 16)
                act.dma_start(prw[0:KC, k, :], x["prT"][rows, :]).then_inc(ld_attn, 16)
            act.dma_start(rw0[KC:KC + 1, 1, :], x["rb0"]).then_inc(ld_rt, 16)
            act.dma_start(gb[:, :, :], x["gb"]).then_inc(ld_rt, 16)
            act.dma_start(prw[KC:KC + 1, 1, :], x["prb"]).then_inc(ld_attn, 16)

            act.wait_ge(ld_con, 16)

            def ln_std(n, g):
                w, m = ln_sem(n, g)
                js = ln_cols(n, g)
                act.wait_ge(var_ready[w], m)
                nc.scalar.activation(std[:, js], mv[:, js, 1], ACT.Sqrt,
                                     bias=con[:, C_EPS:C_EPS + 1]).then_inc(std_ready[w], 1)

            def ln_norm(n, g, src):
                w, m = ln_sem(n, g)
                act.wait_ge(rstd_ready[w], m)
                done = xn_ready if n < 5 else xn5_ready
                for j, i in zip(GROUPS[n][g], range(NJ)[ln_cols(n, g)]):
                    nc.scalar.activation(xn[:, j, :], src[:, j, :], ACT.Identity,
                                         bias=nmr[:, i:i + 1], scale=rstd[:, i:i + 1]).then_inc(done, 1)

            def ln(n):
                for g in range(3):
                    ln_std(n, g)
                for g in range(3):
                    ln_norm(n, g, h)

            ln(1)

            for g in range(3):
                for cc in range(4):
                    u = 4 * g + cc
                    act.wait_ge(proj_mm, u + 1)
                    ps = bank[2 + u % 6]
                    if g == 0:
                        halves = [(0, 0, 0, NPATCH), (1, 256, 0, NPATCH)]
                    else:
                        halves = [(g - 1, 0, NPATCH, T)]
                    for k, (hf, col, t0, t1) in enumerate(halves):
                        n = NCH * (t1 - t0)
                        pr = slice(64 * hf, 64 * hf + 64)
                        if cc == 0:
                            ins = nc.scalar.activation(
                                dec[pr, :, t0:t1], ps[pr, col:col + n].rearrange("p (a t) -> p a t", a=NCH),
                                ACT.Sigmoid)
                        else:
                            ins = nc.scalar.activation(
                                Mt[pr, t0:t1, :, cc - 1, 3].rearrange("p t a -> p a t"),
                                ps[64:128, col:col + n].rearrange("p (a t) -> p a t", a=NCH), ACT.Copy)
                    ins.then_inc(ev_act, 1)
                if g == 0:
                    trig_of(act, link, 0)
            for c in range(1, NCHUNK):
                act.wait_ge(m_ready, c)
                trig_of(act, link, c)

            def experts(l, func, hid):
                def copy_g(iv, s):
                    nc.scalar.activation(gidx[:, s:s + 1], idxs[:, bass.ds(iv * RING + s, 1)],
                                         ACT.Copy).then_inc(gidx_ready, 1)

                def copy_s(iv, s, first=False):
                    if not first:
                        act.wait_ge(scat[s], 16 * (per[s] * l + iv))
                    nc.scalar.activation(sidx[:, s:s + 1], idxs[:, bass.ds(iv * RING + s, 1)],
                                         ACT.Copy).then_inc(sidx_ready, 1)

                def nonlin(i, p):
                    act.wait_ge(g1_mm, l * NT + i + 1)
                    if hid == HID0:
                        nc.scalar.activation(hact[:, 0:hid], bank[2][:, 0:hid], func).then_inc(act_done, 1)
                    else:
                        half = hid // 2
                        nc.scalar.activation(hT2[:, p, 0:half], bank[2 + 2 * p][:, 0:half], func)
                        nc.scalar.activation(hT2[:, p, half:hid], bank[3 + 2 * p][:, 0:half],
                                             func).then_inc(act_done, 1)

                def copy_w(i, p):
                    e = act.value_load(et[0:1, bass.ds(i, 1)], min_val=0, max_val=NE - 1)
                    nc.scalar.activation(w1r[:, p, 1, :],
                                         w1b.rearrange("p e k f -> p (e k f)")[
                                             :, bass.ds(e * (NK * HID1) + HID1, HID1)],
                                         ACT.Copy).then_inc(w1r_act, 1)

                per = [sum(1 for i in range(NT) if i % RING == s) for s in range(RING)]
                act.wait_ge(route_done, l + 1)
                if l:
                    for s in range(RING):
                        act.wait_ge(scat[s], 16 * per[s])
                for s in range(RING):
                    copy_g(0, s)
                if l:
                    act.wait_ge(ld_ffn1, 16 * 2 * NE)
                    copy_w(0, 0)
                    copy_w(1, 1)
                nonlin(0, 0)

                def step(iv, s, first=False, g=True, more=True):
                    if g:
                        copy_g(iv + 1, s)
                    copy_s(iv, s, first=first)
                    if l and not (isinstance(iv, int) and iv * RING + s + 2 >= NT):
                        copy_w(iv * RING + s + 2, s % 2)
                    if more:
                        nonlin(iv * RING + s + 1, (s + 1) % 2)

                for s in range(RING):
                    step(0, s, first=True)
                last = NT // RING - 1
                with act.Fori(1, last) as iv:
                    for s in range(RING):
                        step(iv, s)
                for s in range(RING):
                    step(last, s, g=(last + 1) * RING + s < NT)
                for s in range(NT - (last + 1) * RING):
                    step(last + 1, s, g=False, more=(last + 1) * RING + s + 1 < NT)

            ln(2)
            act.wait_ge(ex_in, 1)
            nc.scalar.activation(ex[:, :, :], ex[:, :, :], ACT.Exp).then_inc(ex_out, 1)
            experts(0, ACT.Gelu, HID0)

            ln(3)
            for u in range(NJ // 2):
                act.wait_ge(kv_mm, u + 1)
                nc.scalar.activation(vb[:, 4 * u:4 * u + 4, 0:KC],
                                     bank[4 + u % 2][:, 0:2 * D].rearrange("p (a n) -> p a n", a=4),
                                     ACT.Copy).then_inc(v_ev, 1)

            def att_evac(i):
                act.wait_ge(at_mm, i + 1)
                t = NPJ + 2 * i
                nc.scalar.activation(attT[0:KC, :, t * P:(t + 2) * P],
                                     bank[5][0:KC, :].rearrange("p (g t) -> p g t", g=NK), ACT.Copy).then_inc(at_ev, 1)
                nc.scalar.activation(attT[0:KC, :, i * P:(i + 1) * P],
                                     bank[6][0:KC, 0:2 * P].rearrange("p (g t) -> p g t", g=NK),
                                     ACT.Copy).then_inc(at_ev, 1)

            att_evac(0)
            ln_std(4, 0)
            att_evac(1)
            for i in range(NBP):
                if i + 1 < NBP:
                    ln_norm(4, i, h)
                    ln_std(4, i + 1)
                    if i + 2 < NBP:
                        att_evac(i + 2)
                    ln_std(5, i)
                    ln_norm(5, i, xn)
                else:
                    ln_norm(4, i, h)
                    ln_std(5, i)
                    ln_norm(5, i, xn)

            act.wait_ge(ex_in, 2)
            nc.scalar.activation(ex[:, :, :], ex[:, :, :], ACT.Exp).then_inc(ex_out, 1)
            experts(1, ACT.Silu, HID1)

        @block.vector
        def _(dve):
            link = Chain(dve, dve_self)
            V = nc.vector
            V.memset(xT[KC:KC + 1, 1, :], 1.0)
            V.memset(xTs[KC:KC + 1, :, 1, :], 1.0).then_inc(ones_ready, 1)

            dve.wait_ge(ld_lab, 16)
            dve.wait_ge(ld_con, 16)
            link(V.tensor_scalar(lab2, lab, 0, NSEG, ALU.is_lt, ALU.mult))
            link(V.tensor_tensor(lab3, lab, lab2, ALU.add))
            link(V.tensor_scalar(lab2, lab3, 0, NSEG - 1, ALU.max, ALU.min))
            V.tensor_scalar(ohl, lab2, con[0:NSEG, C_PART:C_PART + 1], None, ALU.is_equal).then_inc(ohl_ready, 1)
            dve.wait_ge(ld_ids, 16)
            link(V.tensor_scalar(ids2[:, :], ids[:, :], 0, VOCAB, ALU.is_lt, ALU.mult))
            link(V.tensor_tensor(ids2[:, :], ids[:, :], ids2[:, :], ALU.add))
            V.tensor_scalar(ids2[:, :], ids2[:, :], 0, VOCAB - 1, ALU.max, ALU.min).then_inc(ids_ready, 1)
            dve.wait_ge(ld_pos, 64)
            link(V.tensor_tensor(bp[:, 0, :], bp[:, 0, :], bp[:, 1, :], ALU.add))
            for q in range(2):
                dve.wait_ge(patch_mm, q + 1)
                last = V.tensor_tensor(h[:, 2 * q:2 * q + 2, :],
                                       bank[q][:, 0:2 * D].rearrange("p (a n) -> p a n", a=2),
                                       bp[:, 0:1, :].to_broadcast([P, 2, D]), ALU.add)
            for q in range(4):
                dve.wait_ge(seg_mm, q + 1)
                last = V.tensor_tensor(h[:, NPJ + 2 * q:NPJ + 2 * q + 2, :],
                                       bank[2 + q][:, 0:2 * D].rearrange("p (a n) -> p a n", a=2),
                                       sinpos[:, :].unsqueeze(1).to_broadcast([P, 2, D]), ALU.add)
            link(last)
            for q in range(4):
                dve.wait_ge(gath[q], 32)
                js = slice(NPJ + 2 * q, NPJ + 2 * q + 2)
                last = V.tensor_tensor(h[:, js, :], h[:, js, :], xn[:, js, :], ALU.add)
            link(last)

            def ln_start(n, g, src):
                w, _ = ln_sem(n, g)
                cols = list(zip(GROUPS[n][g], range(NJ)[ln_cols(n, g)]))
                for j, i in cols:
                    last = V.bn_stats(st[:, i, :], src[:, j, :])
                link(last)
                for j, i in cols:
                    last = V.bn_aggr(mv[:, i, :], st[:, i, :])
                last.then_inc(var_ready[w], 1)

            def ln_end(n, g):
                w, m = ln_sem(n, g)
                js = ln_cols(n, g)
                dve.wait_ge(std_ready[w], m)
                link(V.reciprocal(rstd[:, js], std[:, js]))
                V.scalar_tensor_tensor(out=nmr[:, js], in0=mv[:, js, 0], scalar=-1.0, in1=rstd[:, js],
                                       op0=ALU.mult, op1=ALU.mult).then_inc(rstd_ready[w], 1)

            def ln(n):
                for g in range(3):
                    ln_start(n, g, h)
                    if g:
                        ln_end(n, g - 1)
                ln_end(n, 2)

            def xt_evac(n):
                m = XT_PASS[n]
                for q in range(NPAIR):
                    dve.wait_ge(xt_psum, m * NPAIR + q + 1)
                    src = bank[q % 2][0:KC, :].rearrange("p (k t) -> p k t", k=NK)
                    dst = xT[0:KC, :, 256 * q:256 * q + 256]
                    V.tensor_copy(dst, src).then_inc(xT_ready, 1)

            V.tensor_copy(iotab[:, :], iota)
            for v in range(2):
                V.tensor_copy(valb[:, v], con[:, C_TOK + v * NJ:C_TOK + (v + 1) * NJ].unsqueeze(1).to_broadcast([P, 2, NJ]))
            ln(1)
            xt_evac(1)
            V.memset(hist, 1.0)
            link(V.memset(prod, 0.0))
            link(V.memset(hist[:, 0, :, 0:3], 0.0))

            for g in range(3):
                for c in range(3):
                    u = 4 * g + c + 1
                    dve.wait_ge(proj_mm, u + 1)
                    ps = bank[2 + u % 6]
                    if g == 0:
                        halves = [(0, 0, 0, NPATCH), (1, 256, 0, NPATCH)]
                    else:
                        halves = [(g - 1, 0, NPATCH, T)]
                    for hf, col, t0, t1 in halves:
                        n = NCH * (t1 - t0)
                        ins = V.tensor_copy(biv[64 * hf:64 * hf + 64, c, :, t0:t1],
                                            ps[0:64, col:col + n].rearrange("p (a t) -> p a t", a=NCH))
                    ins.then_inc(ev_dve, 1)
                if g == 0:
                    prep_angle(dve, V, link, 0)
                    recip_of(dve, V, link, 0)

            dve.wait_ge(ev_act, 4)
            prep_matrix(dve, V, link, 0)

            def steps(t0, n):
                def one(t, k):
                    if k:
                        dve.wait_ge(scan_self, k)
                    V.tensor_tensor(prod.rearrange("p (a r c) -> p a r c", a=NCH, r=3), Mt[:, t],
                                    hist[:, t].unsqueeze(2).to_broadcast([P, NCH, 3, 4]),
                                    ALU.mult).then_inc(scan_self, 1)
                    dve.wait_ge(scan_self, k + 1)
                    V.tensor_reduce(hist[:, t + 1, :, 0:3],
                                    prod.rearrange("p (a r c) -> p a r c", a=NCH, r=3),
                                    AX, ALU.add).then_inc(scan_self, 1)

                for t in range(t0, t0 + n):
                    one(t, 2 * t)

            for c in range(NCHUNK):
                if c:
                    dve.wait_ge(m_ready, c + 1)
                    dve.wait_ge(ev_act, 12)
                steps(c * TCH, TCH // 2)
                if c + 1 < NCHUNK:
                    recip_of(dve, V, link, c + 1)
                steps(c * TCH + TCH // 2, TCH // 2)
            dve.wait_ge(scan_self, 2 * T)
            dve.sem_inc(scanned, 1)

            for q in range(2):
                dve.wait_ge(back_mm, q + 1)
                hv = h[:, q:q + 3:2, :].rearrange("p a (n c) -> p a c n", c=3)
                last = V.tensor_tensor(hv, hv, bank[q][:, 0:384].rearrange("p (c a n) -> p a c n", c=3, a=2), ALU.add)
            for ch in range(NCH):
                dve.wait_ge(back_mm, 3 + ch)
                hv = h[:, NPJ + ch:NPJ + ch + 5:4, :].rearrange("p a (n c) -> p a c n", c=3)
                last = V.tensor_tensor(hv, hv, bank[2 + ch][:, 0:384].rearrange("p (c a n) -> p a c n", c=3, a=2),
                                       ALU.add)
            link(last)
            dve.sem_inc(h_ready, 2)

            def route(l):
                b12, b8 = [P, NJ, NE], [P, NE, NJ]
                dve.wait_ge(zero_done, 16 * 4)
                grp = GROUPS[2] if l == 0 else GROUPS[5]
                for g, js in enumerate(grp):
                    dve.wait_ge(lg_mm, 3 * l + g + 1)
                    ps = bank[LG_BANK[g]][:, 0:len(js) * NE].rearrange("p (j e) -> p j e", e=NE)
                    if l == 0:
                        link(V.tensor_copy(lgs[:, js[0]:js[-1] + 1, :], ps))
                    else:
                        V.tensor_copy(lgs[:, js[0]:js[0] + 1, :], ps[:, 0:1])
                        link(V.tensor_copy(lgs[:, js[1]:js[2] + 1, :], ps[:, 1:3]))
                    for j in js:
                        last = V.max(mx[:, j, :], lgs[:, j, :])
                    link(last)
                    for j in js:
                        last = V.max_index(ix[:, j, :], mx[:, j, :], lgs[:, j, :])
                    if g == len(grp) - 1:
                        link(last)
                m0 = mx[:, :, 0:1]
                V.tensor_tensor(ex[:, :, 0:NE], lgs[:, :, :], m0.to_broadcast(b12), ALU.subtract)
                V.tensor_tensor(ex[:, :, NE:NE + 2], mx[:, :, 0:2], m0.to_broadcast([P, NJ, 2]),
                                ALU.subtract).then_inc(ex_in, 1)
                link(V.tensor_copy(idxf[:, :, :], ix[:, :, 0:2]))
                for k in range(2):
                    last = V.tensor_tensor(oh[:, k], iota[:, 0:NE].unsqueeze(1).to_broadcast(b12),
                                           idxf[:, :, k:k + 1].to_broadcast(b12), ALU.is_equal)
                link(last)
                V.tensor_tensor(msk[:, :, :], oh[:, 0], oh[:, 1], ALU.add).then_inc(msk_ready, 1)
                dve.wait_ge(ex_out, l + 1)
                link(V.tensor_reduce(sm[:, 0, :], ex[:, :, 0:NE], AX, ALU.add))
                link(V.reciprocal(sm[:, 1, :], sm[:, 0, :]))
                link(V.tensor_tensor(gate[:, :, :], ex[:, :, NE:NE + 2].rearrange("p j k -> p k j"),
                                     sm[:, 1:2, :].to_broadcast([P, 2, NJ]), ALU.mult))
                if l == 1:
                    link(V.tensor_tensor(sm[:, 0, :], gate[:, 0, :], gate[:, 1, :], ALU.add))
                    link(V.reciprocal(sm[:, 1, :], sm[:, 0, :]))
                    link(V.tensor_tensor(gate[:, :, :], gate[:, :, :],
                                         sm[:, 1:2, :].to_broadcast([P, 2, NJ]), ALU.mult))
                dve.sem_inc(gate_ready, 1)
                tot, cum, rs = rt[:, 0, :], rt[:, 1, :], con[:, C_RST:C_RST + NE * NJ]
                totv = tot.rearrange("p (e j) -> p e j", e=NE)
                cumv = cum.rearrange("p (e j) -> p e j", e=NE)
                dve.wait_ge(rank_mm, l + 1)
                link(V.tensor_copy(totv, bank[7][:, 192:288].rearrange("p (j e) -> p e j", j=NJ)))
                link(V.tensor_tensor_scan(cum, rs, tot, 0.0, ALU.mult, ALU.add))
                cmpv = rt[:, 2, :].rearrange("p (e j) -> p e j", e=NE)
                link(V.tensor_tensor(cmpv, cumv[:, :, NJ - 1:NJ].to_broadcast(b8),
                                     con[:, C_THR:C_THR + NJ].unsqueeze(1).to_broadcast(b8), ALU.is_gt))
                link(V.tensor_reduce(te[:, 0, :], cmpv, AX, ALU.add))
                link(V.tensor_tensor_scan(te[:, 1, :], con[:, C_ONE:C_ONE + NE], te[:, 0, :], 0.0, ALU.mult, ALU.add))
                link(V.tensor_tensor(te[:, 2, :], te[:, 1, :], te[:, 0, :], ALU.subtract))
                link(V.tensor_scalar(te[:, 3, :], te[:, 2, :], float(P), None, ALU.mult))
                link(V.tensor_tensor(cumv, cumv, totv, ALU.subtract))
                link(V.tensor_tensor(cumv, cumv, te[:, 3, :].unsqueeze(2).to_broadcast(b8), ALU.add))
                slv = rt[:, 2, :].rearrange("p (j e) -> p j e", j=NJ)
                link(V.tensor_tensor(slv, bank[7][:, 96:192].rearrange("p (j e) -> p j e", j=NJ),
                                     cumv.rearrange("p e j -> p j e"), ALU.add))
                for k in range(2):
                    link(V.tensor_tensor(rt[:, 3, :].rearrange("p (j e) -> p j e", j=NJ), oh[:, k], slv, ALU.mult))
                    link(V.tensor_reduce(slf[:, 0, k * NJ:(k + 1) * NJ],
                                         rt[:, 3, :].rearrange("p (j e) -> p j e", j=NJ), AX, ALU.add))
                link(V.tensor_copy(sli[:, 0, :], slf[:, 0, :]))
                V.tensor_scalar(sli[:, 1, :], sli[:, 0, :], 7, None, ALU.arith_shift_right)
                link(V.tensor_scalar(sli[:, 2, :], sli[:, 0, :], P - 1, None, ALU.bitwise_and))
                V.tensor_copy(tileb[:, :], sli[:, 1, :])
                link(V.tensor_copy(slf[:, 2, :], sli[:, 2, :]))
                dve.sem_inc(slot_ready, 1)
                bq = [P, NA, 32]
                link(V.tensor_tensor(oneT, iotab[:, 0:32].unsqueeze(1).to_broadcast(bq),
                                     tileb[:, :].unsqueeze(2).to_broadcast(bq), ALU.is_equal))
                dve.wait_ge(gpart_ready, l + 1)
                for v in range(NV):
                    ins = V.tensor_tensor(oneB[:, :, v, :], oneT,
                                          valb[:, v].rearrange("p k j -> p (k j)").unsqueeze(2).to_broadcast(bq),
                                          ALU.mult)
                ins.then_inc(oneB_ready, 1)
                for a in range(NAP, NA):
                    V.tensor_scalar(oneA[:, a, :], iotab[:, :], slf[:, 2, a:a + 1], None,
                                    ALU.is_equal).then_inc(one_ready, 1)
                be = [1, 32, NE]
                ev = rt[0:1, 0:3, :].rearrange("p a n -> p (a n)")[:, 0:32 * NE].rearrange("p (i e) -> p i e", e=NE)
                link(V.tensor_tensor(ev, iota[0:1, 0:32].unsqueeze(2).to_broadcast(be),
                                     te[0:1, 1, :].unsqueeze(1).to_broadcast(be), ALU.is_ge))
                link(V.tensor_reduce(etf[:, 0, :], ev, AX, ALU.add))
                link(V.tensor_scalar(etf[:, 1, :], etf[:, 0, :], float(NE - 1), None, ALU.min))
                link(V.tensor_copy(et[:, :], etf[:, 1, :]))
                dve.wait_ge(inv_mm, l + 1)
                inv = bank[6][:, 0:NV * 32].rearrange("p (v q) -> p q v", v=NV)
                V.tensor_reduce(gs[:, :], inv[:, :, 2:NV], AX, ALU.add)
                link(V.tensor_reduce(rt[:, 1, 0:32], inv[:, :, 0:2], AX, ALU.add))
                link(V.tensor_scalar(rt[:, 0, 0:32], rt[:, 1, 0:32], 0.0, con[:, C_PAD:C_PAD + 1],
                                     ALU.is_equal, ALU.mult))
                link(V.scalar_tensor_tensor(out=idxs[:, :], in0=rt[:, 1, 0:32], scalar=-1.0,
                                            in1=rt[:, 0, 0:32], op0=ALU.add, op1=ALU.add))
                dve.sem_inc(route_done, 1)

            def experts(l, hid, hc):
                nhc = hid // hc
                per = [sum(1 for i in range(NT) if i % RING == s) for s in range(RING)]

                def evac_x(i, p):
                    dve.wait_ge(tx_mm, l * NT + i + 1)
                    dst = xTs[0:KC, p, :, :]
                    src = bank[p][0:KC, 0:2 * P].rearrange("p (k t) -> p k t", k=NK)
                    if l == 0:
                        V.tensor_copy(dst, src).then_inc(tx_ev, 1)
                    else:
                        V.tensor_scalar(dst[:, 0, :], src[:, 0, :], gb[:, 0, 0:1], gb[:, 1, 0:1], ALU.mult, ALU.add)
                        V.tensor_scalar(dst[:, 1, :], src[:, 1, :], gb[:, 0, 1:2], gb[:, 1, 1:2],
                                        ALU.mult, ALU.add).then_inc(tx_ev, 1)

                def copy_w(i, p):
                    e = dve.value_load(et[0:1, bass.ds(i, 1)], min_val=0, max_val=NE - 1)
                    V.tensor_copy(w1r[:, p, 0, :],
                                  w1b.rearrange("p e k f -> p (e k f)")[:, bass.ds(e * (NK * HID1), HID1)]
                                  ).then_inc(w1r_dve, 1)

                def evac_h(i):
                    dve.wait_ge(th_mm, l * NT + i + 1)
                    V.tensor_copy(hTs[0:hc, 0:nhc * P], bank[4][0:hc, 0:nhc * P]).then_inc(th_ev, 1)

                def evac_y(iv, s, first=False):
                    i = iv * RING + s
                    dve.wait_ge(g2_mm, l * NT + i + 1)
                    if not first:
                        dve.wait_ge(scat[s], 16 * (per[s] * l + iv))
                    V.tensor_scalar(ys[:, s, :], bank[6][:, 0:D], gs[:, bass.ds(i, 1)], None,
                                    ALU.mult).then_inc(y_ev, 1)

                if l:
                    dve.wait_ge(ld_ffn1, 16 * 2 * NE)
                for p in range(2):
                    if l:
                        copy_w(p, p)
                    evac_x(p, p)

                def step(iv, s, first=False, xx=True):
                    if l == 0:
                        evac_h(iv * RING + s)
                    if xx:
                        evac_x(iv * RING + s + 2, s % 2)
                        if l:
                            copy_w(iv * RING + s + 2, s % 2)
                    evac_y(iv, s, first=first)

                for s in range(RING):
                    step(0, s, first=(l == 0))
                last = NT // RING - 1
                with dve.Fori(1, last) as iv:
                    for s in range(RING):
                        step(iv, s)
                for s in range(RING):
                    step(last, s, xx=last * RING + s + 2 < NT)
                for s in range(NT - (last + 1) * RING):
                    step(last + 1, s, xx=(last + 1) * RING + s + 2 < NT)

            def add_acc():
                for p, buf in enumerate((xn, a1)):
                    dve.wait_ge(acc_ld[p], 16 * 3)
                    link(V.tensor_tensor(h[:, :, :], h[:, :, :], buf[:, :, :], ALU.add))

            ln(2)
            xt_evac(2)
            route(0)
            V.memset(hTs[KC:KC + 1, 0:3 * P], 1.0)
            experts(0, HID0, HC0)
            add_acc()

            V.tensor_scalar(xTs[0:KC, 0, 0, :], con[0:KC, C_ONE:C_ONE + P], gb[:, 1, 0:1], None, ALU.mult)
            V.tensor_scalar(xTs[0:KC, 0, 1, :], con[0:KC, C_ONE:C_ONE + P], gb[:, 1, 1:2], None,
                            ALU.mult).then_inc(bb_ready, 1)
            V.tensor_scalar(rwg[0:KC, 0, :], rw1[0:KC, 0, :], gb[:, 0, 0:1], None, ALU.mult)
            V.tensor_scalar(rwg[0:KC, 1, :], rw1[0:KC, 1, :], gb[:, 0, 1:2], None, ALU.mult)
            ln(3)
            V.memset(vb[:, :, KC:KV], 1.0)
            V.memset(attT[KC:KC + 1, 1, :], 1.0)
            xt_evac(3)
            dve.wait_ge(bias_mm, 1)
            V.tensor_copy(rwg[KC:KC + 1, 1, :], bank[7][KC:KC + 1, 0:NE]).then_inc(rwg_ready, 1)

            def kv_evac(u):
                dve.wait_ge(kv_mm, u + 1)
                V.tensor_scalar(kb[:, 2 * u:2 * u + 2, :], bank[2 + u % 2][:, 0:2 * D].rearrange("p (j n) -> p j n", j=2),
                                0.0, float(HD) ** -0.5, ALU.max, ALU.add).then_inc(k_ev, 1)

            def q_evac(u):
                g, m = u // 2, u % 2
                dve.wait_ge(q_mm, u + 1)
                V.tensor_scalar(qT[:, m, 512 * g:512 * g + 512], bank[u % 2 + 6][0:KC, :], 0.0,
                                float(HD) ** -0.5, ALU.max, ALU.add).then_inc(q_ev, 1)

            def state(i):
                dve.wait_ge(st_mm, i + 1)
                if i >= 2:
                    dve.wait_ge(nd_mm, i - 1)
                for a in range(2):
                    ins = V.tensor_tensor(kvm[:, i % 2, 2 * a:2 * a + 2],
                                          bank[a][0:KC, 0:2 * KV].rearrange("p (g n) -> p g n", g=NK),
                                          con[0:KC, C_MASK:C_MASK + KV].unsqueeze(1).to_broadcast([KC, NK, KV]),
                                          ALU.mult)
                ins.then_inc(st_ev, 1)

            def ratio(i):
                dve.wait_ge(nd_mm, i + 1)
                txt = bank[2][:, 0:4 * KV].rearrange("p (a n) -> p a n", a=4)
                pat = bank[3][:, 0:2 * KV].rearrange("p (a n) -> p a n", a=2)
                hg = KC // HD
                zz = z[:, :, :].rearrange("p j (a n) -> p (j a) n", n=hg)
                V.tensor_scalar(zz[:, 2:6], txt[:, :, KC:KV], 1e-6, None, ALU.add)
                link(V.tensor_scalar(zz[:, 0:2], pat[:, :, KC:KV], 1e-6, None, ALU.add))
                link(V.reciprocal(z[:, :, :], z[:, :, :]))
                t = NPJ + 2 * i
                for lo, n, ps, dst in ((0, 2, pat, att[:, i:i + 1, :]), (2, 4, txt, att[:, t:t + 2, :])):
                    V.tensor_tensor(dst.rearrange("p j (a n e) -> p (j a) n e", n=hg, e=HD),
                                    ps[:, :, 0:KC].rearrange("p a (n e) -> p a n e", e=HD),
                                    zz[:, lo:lo + n].unsqueeze(3).to_broadcast([P, n, hg, HD]),
                                    ALU.mult).then_inc(att_ready, 1)
                dve.wait_ge(att_ready, 2 * i + 2)

            def add_att(i):
                dve.wait_ge(pr_mm, i + 1)
                t = NPJ + 2 * i
                V.tensor_tensor(h[:, i, :], h[:, i, :], bank[4][:, 0:D], ALU.add).then_inc(h_ready, 1)
                V.tensor_tensor(h[:, t:t + 2, :], h[:, t:t + 2, :],
                                bank[7][:, 0:2 * D].rearrange("p (j n) -> p j n", j=2), ALU.add).then_inc(h_ready, 1)
                dve.wait_ge(h_ready, 2 + 2 * i + 2)
                ln_start(4, i, h)

            def residual(i):
                dve.wait_ge(xn_ready, 3 * NJ + 3 * i + 3)
                t = NPJ + 2 * i
                ln_start(5, i, xn)
                V.tensor_tensor(h[:, i, :], h[:, i, :], xn[:, i, :], ALU.add)
                V.tensor_tensor(h[:, t:t + 2, :], h[:, t:t + 2, :], xn[:, t:t + 2, :], ALU.add).then_inc(res_done, 1)

            def xt5_evac(i):
                dve.wait_ge(xt5_mm, i + 1)
                t = NPJ + 2 * i
                b0, b1 = (bank[0], bank[2]) if i % 2 == 0 else (bank[3], bank[1])
                V.tensor_copy(xT[0:KC, :, t * P:(t + 2) * P], b0[0:KC, :].rearrange("p (k t) -> p k t", k=NK))
                V.tensor_copy(xT[0:KC, :, i * P:(i + 1) * P],
                              b1[0:KC, 0:2 * P].rearrange("p (k t) -> p k t", k=NK)).then_inc(xT5_ready, 1)

            for g in range(2):
                kv_evac(2 * g)
                kv_evac(2 * g + 1)
                q_evac(2 * g)
                q_evac(2 * g + 1)
            state(0)
            kv_evac(4)
            kv_evac(5)
            ratio(0)
            state(1)
            q_evac(4)
            q_evac(5)
            ratio(1)
            state(2)
            add_att(0)
            ratio(2)
            state(3)
            ln_end(4, 0)
            add_att(1)
            ratio(3)
            residual(0)
            ln_end(4, 1)
            ln_end(5, 0)
            add_att(2)
            residual(1)
            ln_end(4, 2)
            ln_end(5, 1)
            add_att(3)
            residual(2)
            ln_end(4, 3)
            ln_end(5, 2)
            xt5_evac(0)
            residual(3)
            xt5_evac(1)
            ln_end(5, 3)
            xt5_evac(2)
            xt5_evac(3)

            route(1)
            experts(1, HID1, HC1)

        @block.tensor
        def _(pe):
            MM = nc.tensor.matmul

            def rows(k, biased=True):
                return KC + 1 if (k == NK - 1 and biased) else KC

            pe.wait_ge(ld_con, 16)
            pe.wait_ge(ld_patch, 32)
            for q in range(2):
                for jj in range(2):
                    j = 2 * q + jj
                    for k in range(4):
                        ins = MM(bank[q][:, jj * D:(jj + 1) * D], patchT[:, k, j * P:(j + 1) * P], projT[:, k, :],
                                 start=(k == 0), stop=(k == 3))
                ins.then_inc(patch_mm, 1)
            pe.wait_ge(ohl_ready, 1)
            pe.wait_ge(ld_seg, 16)
            for q in range(4):
                for jj in range(2):
                    b = 2 * q + jj
                    ins = MM(bank[2 + q][:, jj * D:(jj + 1) * D], ohl[:, b * NTXT:(b + 1) * NTXT], segt[:, :],
                             start=True, stop=True)
                ins.then_inc(seg_mm, 1)

            def t_pair(n, q):
                m = XT_PASS[n]
                pe.wait_ge(xn_ready, (n - 1) * NJ + 2 * q + 2)
                if m * NPAIR + q >= 2:
                    pe.wait_ge(xT_ready, m * NPAIR + q - 1)
                for k in range(NK):
                    for jj in range(2):
                        ins = nc.tensor.transpose(bank[q % 2][0:KC, (2 * k + jj) * P:(2 * k + jj + 1) * P],
                                                  xn[:, 2 * q + jj, k * KC:(k + 1) * KC], ident)
                ins.then_inc(xt_psum, 1)

            def transposes(n):
                for q in range(NPAIR):
                    t_pair(n, q)

            def logits(l, i):
                rw = (rw0, rwg)[l]
                pe.wait_ge(ld_rt, 16 * 6)
                if l == 0:
                    pe.wait_ge(xT_ready, NPAIR + 2 * i + 2)
                    if i == 2:
                        pe.wait_ge(h_ready, 2)
                else:
                    pe.wait_ge(xT5_ready, i + 1)
                for n, j in enumerate(GROUPS[2 if l == 0 else 5][i]):
                    for k in range(NK):
                        r = rows(k)
                        ins = MM(bank[LG_BANK[i]][:, n * NE:(n + 1) * NE], xT[0:r, k, j * P:(j + 1) * P], rw[0:r, k, :],
                                 start=(k == 0), stop=(k == NK - 1))
                ins.then_inc(lg_mm, 1)

            def ranks(l):
                pe.wait_ge(msk_ready, l + 1)
                m = msk[:, :, :].rearrange("p j e -> p (j e)")
                MM(bank[7][:, 96:192], con[:, C_TRI:C_TRI + P], m, start=True, stop=True)
                MM(bank[7][:, 192:288], con[:, C_ONE:C_ONE + P], m, start=True, stop=True).then_inc(rank_mm, 1)
                pe.wait_ge(oneB_ready, l + 1)
                for a in range(NA):
                    if a < NAP:
                        pe.wait_ge(oneP_ready, NAP * l + a + 1)
                    else:
                        pe.wait_ge(one_ready, (NA - NAP) * l + a - NAP + 1)
                    ins = MM(bank[6][:, 0:NV * 32], oneA[:, a, :], oneB[:, a, :, :].rearrange("p v q -> p (v q)"),
                             start=(a == 0), stop=(a == NA - 1))
                ins.then_inc(inv_mm, 1)

            def experts(l, hid, hc, w1, w2, biased):
                nhc = hid // hc
                w1v = w1.rearrange("p e k f -> p (e k f)")
                w2v = w2.rearrange("p e c n -> p (e c n)")

                def expert_of(i):
                    return pe.value_load(et[0:1, bass.ds(i, 1)], min_val=0, max_val=NE - 1)

                def t_x(iv, s):
                    per = sum(1 for i in range(NT) if i % RING == s)
                    i = iv * RING + s
                    pe.wait_ge(xs_ready[s], 16 * (l * per + iv + 1))
                    for k in range(NK):
                        ins = nc.tensor.transpose(bank[s % 2][0:KC, k * P:(k + 1) * P],
                                                  xs[:, s, k * KC:(k + 1) * KC], ident)
                    ins.then_inc(tx_mm, 1)

                def g1(i, p, e):
                    pe.wait_ge(tx_ev, l * NT + i + 1)
                    if l == 0:
                        for k in range(NK):
                            r = rows(k, biased)
                            ins = MM(bank[2][:, 0:hid], xTs[0:r, p, k, :],
                                     w1v[0:r, bass.ds(e * (NK * hid) + k * hid, hid)],
                                     start=(k == 0), stop=(k == NK - 1))
                        ins.then_inc(g1_mm, 1)
                        return
                    pe.wait_ge(w1r_act, i + 1)
                    pe.wait_ge(w1r_dve, i + 1)
                    for c in range(nhc):
                        o_ = bank[2 + 2 * p + c // 3][:, (c % 3) * P:(c % 3 + 1) * P]
                        for k in range(NK):
                            ins = MM(o_, w1r[:, p, k, c * hc:(c + 1) * hc], xTs[0:KC, p, k, :],
                                     start=(k == 0), stop=(k == NK - 1))
                    ins.then_inc(g1_mm, 1)

                def t_h(i):
                    pe.wait_ge(act_done, l * NT + i + 1)
                    for c in range(nhc):
                        ins = nc.tensor.transpose(bank[4][0:hc, c * P:(c + 1) * P], hact[:, c * hc:(c + 1) * hc], ident)
                    ins.then_inc(th_mm, 1)

                def g2(i, p, e):
                    if l == 0:
                        pe.wait_ge(th_ev, i + 1)
                    else:
                        pe.wait_ge(act_done, NT + i + 1)
                    if not (isinstance(i, int) and i == 0 and l == 0):
                        pe.wait_ge(y_ev, l * NT + i)
                    for c in range(nhc):
                        r = hc + 1 if (c == nhc - 1 and biased) else hc
                        ins = MM(bank[6][:, 0:D], (hTs if l == 0 else hT2[:, p])[0:r, c * P:(c + 1) * P],
                                 w2v[0:r, bass.ds(e * (nhc * D) + c * D, D)],
                                 start=(c == 0), stop=(c == nhc - 1))
                    ins.then_inc(g2_mm, 1)

                pe.wait_ge(route_done, l + 1)
                pe.wait_ge(ones_ready, 1)
                pe.wait_ge(ld_ffn0 if l == 0 else ld_ffn1, 16 * (2 * NE + 2) if l == 0 else 16 * 2 * NE)
                t_x(0, 0)
                t_x(0, 1)
                g1(0, 0, expert_of(0))

                def step(iv, s, e, n_left):
                    i = iv * RING + s
                    if n_left > 2:
                        t_x(iv + (s + 2) // RING, (s + 2) % RING)
                    if l == 0:
                        t_h(i)
                    nxt = None
                    if n_left > 1:
                        nxt = expert_of(i + 1)
                        g1(i + 1, (s + 1) % 2, nxt)
                    g2(i, s % 2, e)
                    return nxt

                e = expert_of(0)
                for s in range(RING):
                    e = step(0, s, e, NT)
                last = NT // RING - 1
                with pe.Fori(1, last) as iv:
                    e = expert_of(iv * RING)
                    for s in range(RING):
                        e = step(iv, s, e, NT)
                e = expert_of(last * RING)
                for i in range(last * RING, NT):
                    e = step(i // RING, i % RING, e, NT - i)

            transposes(1)
            pe.wait_ge(ld_wst, 48)
            pe.wait_ge(ones_ready, 1)
            for g in range(3):
                pe.wait_ge(xT_ready, 2 * (g + 1))
                for cc in range(4):
                    u = 4 * g + cc
                    if u < 4:
                        pass
                    if u >= 6:
                        v = u - 6
                        pe.wait_ge(ev_act, v + 1)
                        if v % 4:
                            pe.wait_ge(ev_dve, 3 * (v // 4) + v % 4)
                    for k in range(NK):
                        r = rows(k)
                        ins = MM(bank[2 + u % 6][:, :], wst[0:r, k, cc, :], xT[0:r, k, 512 * g:512 * g + 512],
                                 start=(k == 0), stop=(k == NK - 1))
                    ins.then_inc(proj_mm, 1)
            pe.wait_ge(scanned, 1)
            for q in range(2):
                for c in range(3):
                    for a in range(2):
                        ins = MM(bank[q][NPATCH * a:NPATCH * (a + 1), c * P:(c + 1) * P],
                                 hist[:, 1:NPATCH + 1, 2 * q + a, c], ident, start=True, stop=True)
                ins.then_inc(back_mm, 1)
            for ch in range(NCH):
                for c in range(3):
                    ins = nc.tensor.transpose(bank[2 + ch][:, c * P:(c + 1) * P], hist[:, NPATCH + 1:T + 1, ch, c],
                                              ident)
                ins.then_inc(back_mm, 1)

            for q in range(NPAIR):
                t_pair(2, q)
                if q in (2, 4):
                    logits(0, q // 2 - 1)
            logits(0, 2)
            ranks(0)
            experts(0, HID0, HC0, w1a, w2a, True)

            pe.wait_ge(bb_ready, 1)
            for k in range(NK):
                ins = MM(bank[7][:, 0:NE], xTs[0:KC, 0, k, :], rw1[0:KC, k, :], start=(k == 0), stop=(k == NK - 1))
            ins.then_inc(bias_mm, 1)
            transposes(3)
            pe.wait_ge(ld_attn, 16 * 5)

            def kv_mms(u):
                pe.wait_ge(xT_ready, 2 * NPAIR + u + 1)
                if u >= 2:
                    pe.wait_ge(k_ev, u - 1)
                    pe.wait_ge(v_ev, u - 1)
                for w in range(2):
                    for jj in range(2):
                        j = 2 * u + jj
                        for k in range(NK):
                            ins = MM(bank[2 + 2 * w + u % 2][:, jj * D:(jj + 1) * D], xT[0:KC, k, j * P:(j + 1) * P],
                                     qkvw[:, k, (1 + w) * D:(2 + w) * D], start=(k == 0), stop=(k == NK - 1))
                ins.then_inc(kv_mm, 1)

            def q_mms(u):
                g, m = u // 2, u % 2
                if u >= 2:
                    pe.wait_ge(q_ev, u - 1)
                if u == 1:
                    pe.wait_ge(rwg_ready, 1)
                for k in range(NK):
                    ins = MM(bank[u % 2 + 6][0:KC, :], qkvw[:, k, m * KC:(m + 1) * KC],
                             xT[0:KC, k, 512 * g:512 * g + 512], start=(k == 0), stop=(k == NK - 1))
                ins.then_inc(q_mm, 1)

            def sums(i):
                pe.wait_ge(k_ev, 3 + i)
                pe.wait_ge(v_ev, 3 + i)
                if i == 0:
                    pe.wait_ge(xT_ready, 3 * NPAIR)
                else:
                    pe.wait_ge(st_ev, i)
                for a in range(2):
                    b = 2 * i + a
                    ph = slice(NPATCH * a, NPATCH * a + NPATCH)
                    for g in range(NK):
                        o_ = bank[a][0:KC, g * KV:(g + 1) * KV]
                        MM(o_, kb[:, NPJ + b, g * KC:(g + 1) * KC], vb[:, 2 * (NPJ + b) + g, :], start=True, stop=False)
                        ins = MM(o_, kb[ph, i, g * KC:(g + 1) * KC], vb[ph, 2 * i + g, :], start=False, stop=True)
                ins.then_inc(st_mm, 1)

            def numden(i):
                pe.wait_ge(st_ev, i + 1)
                pe.wait_ge(q_ev, 2 * (1 + i // 2) + 2)
                if i == 0:
                    pe.wait_ge(k_ev, 6)
                    pe.wait_ge(v_ev, 6)
                else:
                    pe.wait_ge(att_ready, 2 * i)
                for a in range(2):
                    for g in range(NK):
                        q0 = P * i + NPATCH * a
                        MM(bank[3][NPATCH * a:NPATCH * (a + 1), g * KV:(g + 1) * KV], qT[:, g, q0:q0 + NPATCH],
                           kvm[:, i % 2, 2 * a + g, :], start=True, stop=True)
                for a in range(2):
                    for g in range(NK):
                        q0 = P * (NPJ + 2 * i + a)
                        ins = MM(bank[2][:, (2 * a + g) * KV:(2 * a + g + 1) * KV], qT[:, g, q0:q0 + P],
                                 kvm[:, i % 2, 2 * a + g, :], start=True, stop=True)
                ins.then_inc(nd_mm, 1)

            def t_trio(src, i, b0, b1):
                for k in range(NK):
                    for a in range(2):
                        nc.tensor.transpose(b0[0:KC, (2 * k + a) * P:(2 * k + a + 1) * P],
                                            src[:, NPJ + 2 * i + a, k * KC:(k + 1) * KC], ident)
                    ins = nc.tensor.transpose(b1[0:KC, k * P:(k + 1) * P], src[:, i, k * KC:(k + 1) * KC], ident)
                return ins

            def t_att(i):
                pe.wait_ge(att_ready, 2 * i + 2)
                if i == 0:
                    pe.wait_ge(q_ev, 6)
                else:
                    pe.wait_ge(at_ev, 2 * i)
                t_trio(att, i, bank[5], bank[6]).then_inc(at_mm, 1)

            def out_proj(i):
                pe.wait_ge(at_ev, 2 * i + 2)
                if i:
                    pe.wait_ge(h_ready, 2 + 2 * i)
                for n, (bk, j) in enumerate(zip((bank[4][:, 0:D], bank[7][:, 0:D], bank[7][:, D:2 * D]), trio(i))):
                    for g in range(NK):
                        ins = MM(bk, attT[0:rows(g), g, j * P:(j + 1) * P], prw[0:rows(g), g, :],
                                 start=(g == 0), stop=(g == NK - 1))
                ins.then_inc(pr_mm, 1)

            for g in range(2):
                kv_mms(2 * g)
                kv_mms(2 * g + 1)
                q_mms(2 * g)
                q_mms(2 * g + 1)
            sums(0)
            kv_mms(4)
            kv_mms(5)
            numden(0)
            sums(1)
            q_mms(4)
            q_mms(5)
            t_att(0)
            numden(1)
            sums(2)
            out_proj(0)
            t_att(1)
            numden(2)
            sums(3)
            out_proj(1)
            t_att(2)
            numden(3)
            out_proj(2)
            t_att(3)
            out_proj(3)
            for i in range(NBP):
                pe.wait_ge(xn5_ready, 3 * i + 3)
                if i == 0:
                    pe.wait_ge(att_ready, 2 * NBP)
                elif i >= 2:
                    pe.wait_ge(xT5_ready, i - 1)
                t_trio(xn, i, *((bank[0], bank[2]) if i % 2 == 0 else (bank[3], bank[1]))).then_inc(xt5_mm, 1)
                if i:
                    logits(1, i - 1)
            logits(1, NBP - 1)

            ranks(1)
            experts(1, HID1, HC1, w1b, w2b, False)


def constants():
    c = np.zeros((P, NCONST), np.float32)
    p = np.arange(P)
    c[:, C_ID:C_ID + P] = np.eye(P)
    c[:, C_TRI:C_TRI + P] = p[:, None] < p[None, :]
    c[:, C_ONE:C_ONE + P] = 1.0
    e = np.arange(KC)
    c[:KC, C_MASK:C_MASK + KC] = e[:, None] // HD == e[None, :] // HD
    c[:KC, C_MASK + KC:C_MASK + KV] = e[:, None] // HD == np.arange(KC // HD)[None, :]
    c[:, C_IOTA:C_IOTA + P] = p[None, :]
    c[:, C_THR:C_THR + NJ] = P * np.arange(NJ)[None, :]
    c[:, C_RST:C_RST + NE * NJ] = (np.arange(NE * NJ) % NJ != 0)[None, :]
    for j in range(NJ):
        if j < NPJ:
            row = (2 * j + p // NPATCH) * T + p % NPATCH
        else:
            row = (j - NPJ) * T + NPATCH + p
        c[:, C_TOK + j] = (row + 1) // 8 * 8
        c[:, C_TOK + NJ + j] = (row + 1) % 8
    c[:, C_PAD] = NTOK + 1 + p
    c[:, C_EPS] = EPS
    c[:, C_HPI] = np.pi / 2
    c[:, C_PART] = p
    pos = np.arange(NTXT, dtype=np.float32)[:, None]
    i = np.arange(D, dtype=np.float32)[None, :]
    angle = pos / np.power(np.float32(10000.0), (np.floor(i / np.float32(2.0)) * np.float32(2.0) / np.float32(D)))
    sinpos = np.where(np.arange(D) % 2 == 0, np.sin(angle), np.cos(angle)).astype(np.float32)
    return c, sinpos


def kernel(**inp):
    import concourse.bacc as bacc
    from concourse.bass_utils import run_bass_kernel_spmd

    a = {k: np.asarray(v) for k, v in inp.items()}
    con, sinpos = constants()
    arr = {"consts": con, "sinpos": sinpos}
    n = 128 // 16
    patches = a["x"].reshape(B, 2, n, 16, n, 16).transpose(0, 1, 2, 4, 3, 5).reshape(B * NPATCH, PD).T
    arr["patchT"] = patches
    arr["projT"] = a["L0_tok_proj_w"].T
    arr["projb"] = a["L0_tok_proj_b"].reshape(D)
    arr["pos"] = a["L0_tok_pos_emb"].reshape(NPATCH, D)
    arr["labels"] = a["mask_BS_i2_0"].reshape(B * NTXT)
    arr["ids"] = a["x_txt"].T
    arr["table"] = a["L0_txt_token_table"]
    arr["segm"] = a["L0_txt_segm_table"]
    wb = a["L0_attn_W_biv"].reshape(NB, 3, D).transpose(2, 1, 0)
    wi = a["L0_attn_W_in"].reshape(NB, 3, D).transpose(2, 1, 0)
    wd = np.repeat(a["L0_attn_W_decay"].T, P, axis=1).reshape(D, 1, P)
    arr["wst"] = np.concatenate([wd, np.concatenate([wb, wi], axis=2)], axis=1)
    bb = a["L0_attn_b_biv"].reshape(NB, 3).T
    bi = a["L0_attn_b_in"].reshape(NB, 3).T
    bd = np.repeat(a["L0_attn_b_decay"], P).reshape(1, P)
    arr["wst_b"] = np.concatenate([bd, np.concatenate([bb, bi], axis=1)], axis=0)[None]
    arr["rw0"], arr["rb0"] = a["L0_ffn_router_w"], a["L0_ffn_router_b"].reshape(1, NE)
    arr["w1a"], arr["b1a"] = a["L0_ffn_w1"], a["L0_ffn_b1"]
    arr["w2a"], arr["b2a"] = a["L0_ffn_w2"], a["L0_ffn_b2"]
    arr["qkvT"], arr["prT"] = a["L1_attn_qkv_w"].T, a["L1_attn_proj_w"].T
    arr["prb"] = a["L1_attn_proj_b"].reshape(1, D)
    g = a["L1_ffn_ln_gamma"].reshape(NK, KC).T
    be = a["L1_ffn_ln_beta"].reshape(NK, KC).T
    arr["gb"] = np.stack([g, be], axis=1)
    arr["rw1"] = a["L1_ffn_router_w"]
    arr["w1b"], arr["w2b"] = a["L1_ffn_w1"], a["L1_ffn_w2"]

    nc = bacc.Bacc("TRN2", target_bir_lowering=False, num_devices=1)
    arrays, aps = {}, {}
    for k, v in arr.items():
        v = np.ascontiguousarray(v)
        arrays["in_" + k] = v
        aps[k] = nc.dram_tensor("in_" + k, v.shape, mybir.dt.from_np(v.dtype), kind="ExternalInput").ap()
    out = nc.dram_tensor("out", (ROWS, D), F32, kind="ExternalOutput").ap()
    build(nc, aps, out)
    r = run_bass_kernel_spmd(nc, [arrays], core_ids=[0])
    return r.results[0]["out"][0:NTOK].reshape(B, T, D)
```
